# Optimizing a Trainium2 kernel written in Bass

```python
import numpy as np
import jax
import jax.numpy as jnp

def _softmax(x, axis=-1):
    return jax.nn.softmax(x, axis=axis)

def _gelu(x):
    return jax.nn.gelu(x, approximate=True)

def _silu(x):
    return jax.nn.silu(x)

def _sigmoid(x):
    return jax.nn.sigmoid(x)

def _layernorm(x, axis=-1, eps=1e-05):
    m = jnp.mean(x, axis=axis, keepdims=True)
    v = jnp.var(x, axis=axis, keepdims=True)
    return (x - m) / jnp.sqrt(v + eps)

def _scatter_add(tgt, idx, src, axis=0):
    return tgt.at[idx].add(src)

def _segment_sum(src, seg, n):
    return jax.ops.segment_sum(src, seg, n)
kernel_name = 'mk_perceiver_d1_seqx_r8_f74ceb'

def setup_inputs(seed: int=0):
    np.random.seed(seed)
    _w = jnp.asarray

    def _rec_inputs():
        import jax
        import jax.numpy as jnp
        _rk = jax.random.key(seed)
        x = 7.22e-05 + 1 * jax.random.normal(jax.random.fold_in(_rk, 1), (128, 32, 128), jnp.float32)
        _lenS = 32 - jax.random.randint(jax.random.fold_in(_rk, 7), (128,), 0, max(1, 32 // 4) + 1, jnp.int32)
        _lenS2 = 257 - jax.random.randint(jax.random.fold_in(_rk, 8), (128,), 0, max(1, 257 // 4) + 1, jnp.int32)
        _ctx_1024P = jax.random.normal(jax.random.fold_in(_rk, 11), (128, 16, 128), jnp.float32)
        _ctx_1024c = jax.random.dirichlet(jax.random.fold_in(_rk, 511), 0.3 * jnp.ones((16,), jnp.float32), (128, 257))
        _ctx_1024t = jnp.einsum('bsk,bkd->bsd', _ctx_1024c, _ctx_1024P)
        _ctx_1024t = _ctx_1024t * jax.lax.rsqrt(jnp.mean(jnp.square(_ctx_1024t)) + 1e-12) * 0.953939
        ctx_1024 = 4.13588e-05 + 0.999923 * (_ctx_1024t + 0.3 * jax.random.normal(jax.random.fold_in(_rk, 611), (128, 257, 128), jnp.float32))
        _validS = jnp.arange(32)[None, :] < _lenS[:, None]
        _validS2 = jnp.arange(257)[None, :] < _lenS2[:, None]
        _causal = jnp.tril(jnp.ones((32, 32), dtype=bool))
        mask_BxSxS2_ik1 = jnp.where(jnp.broadcast_to(_validS2[:, None, :], (128, 32, 257)), 1, 0).astype(jnp.int32)
        return (x, ctx_1024, mask_BxSxS2_ik1)
    x, ctx_1024, mask_BxSxS2_ik1 = _rec_inputs()

    def _L0_xattn_setup():
        import jax, jax.numpy as jnp
        import numpy as np
        HID = 128
        HEADS = 16
        HEAD_DIM = HID // HEADS

        def _split_heads(x, W, b):
            B, S, _ = x.shape
            y = x @ W + b
            return y.reshape(B, S, HEADS, HEAD_DIM).transpose(0, 2, 1, 3)
        key = jax.random.key(seed)
        ks = jax.random.split(key, 12)
        B, S = (4, 256)
        inp = {'query': jax.random.normal(ks[0], (B, S, HID), dtype=jnp.float32), 'key': jax.random.normal(ks[1], (B, S, HID), dtype=jnp.float32), 'value': jax.random.normal(ks[2], (B, S, HID), dtype=jnp.float32), 'mask': jax.random.randint(ks[3], (B, S, S), 0, 2, dtype=jnp.int32), 'Wq': jax.random.normal(ks[4], (HID, HID), dtype=jnp.float32) * (1.0 / np.sqrt(HID)), 'bq': jnp.zeros((HID,), dtype=jnp.float32), 'Wk': jax.random.normal(ks[5], (HID, HID), dtype=jnp.float32) * (1.0 / np.sqrt(HID)), 'bk': jnp.zeros((HID,), dtype=jnp.float32), 'Wv': jax.random.normal(ks[6], (HID, HID), dtype=jnp.float32) * (1.0 / np.sqrt(HID)), 'bv': jnp.zeros((HID,), dtype=jnp.float32), 'Wo': jax.random.normal(ks[7], (HID, HID), dtype=jnp.float32) * (1.0 / np.sqrt(HID)), 'bo': jnp.zeros((HID,), dtype=jnp.float32)}
        return inp
    _L0_xattn_all = _L0_xattn_setup()
    _L0_xattn_in = {k: v for k, v in _L0_xattn_all.items() if k in ('Wq', 'bq', 'Wk', 'bk', 'Wv', 'bv', 'Wo', 'bo')}
    del _L0_xattn_all

    def _L0_attn_setup():
        import jax, jax.numpy as jnp
        import numpy as np
        D_MODEL = 128
        N_HEAD = 16
        N_KV_HEAD = 4
        HEAD_DIM = D_MODEL // N_HEAD
        N_GROUP = N_HEAD // N_KV_HEAD
        ROPE_BASE = 10000.0
        ROPE_DIM = HEAD_DIM

        def _rope_tables(seq_len, dtype):
            half = ROPE_DIM // 2
            inv_freq = 1.0 / ROPE_BASE ** (jnp.arange(0, half, dtype=jnp.float32) * 2.0 / ROPE_DIM)
            pos = jnp.arange(seq_len, dtype=jnp.float32)
            freqs = pos[:, None] * inv_freq[None, :]
            return (jnp.cos(freqs).astype(dtype), jnp.sin(freqs).astype(dtype))

        def _apply_rope(t):
            S = t.shape[2]
            cos, sin = _rope_tables(S, t.dtype)
            half = ROPE_DIM // 2
            t1 = t[..., :half]
            t2 = t[..., half:ROPE_DIM]
            rot = jnp.concatenate([t1 * cos - t2 * sin, t1 * sin + t2 * cos], axis=-1)
            if ROPE_DIM < t.shape[-1]:
                rot = jnp.concatenate([rot, t[..., ROPE_DIM:]], axis=-1)
            return rot
        key = jax.random.key(seed)
        ks = jax.random.split(key, 5)
        B, S = (1, 512)
        sd = 1.0 / np.sqrt(D_MODEL)
        x = jax.random.normal(ks[0], (B, S, D_MODEL), dtype=jnp.float32)
        w_q = jax.random.normal(ks[1], (D_MODEL, N_HEAD * HEAD_DIM), dtype=jnp.float32) * sd
        w_k = jax.random.normal(ks[2], (D_MODEL, N_KV_HEAD * HEAD_DIM), dtype=jnp.float32) * sd
        w_v = jax.random.normal(ks[3], (D_MODEL, N_KV_HEAD * HEAD_DIM), dtype=jnp.float32) * sd
        w_o = jax.random.normal(ks[4], (D_MODEL, D_MODEL), dtype=jnp.float32) * sd
        return {'x': x, 'w_q': w_q, 'w_k': w_k, 'w_v': w_v, 'w_o': w_o}
    _L0_attn_all = _L0_attn_setup()
    _L0_attn_in = {k: v for k, v in _L0_attn_all.items() if k in ('w_q', 'w_k', 'w_v', 'w_o')}
    del _L0_attn_all

    def _L0_ffn_setup():
        import jax, jax.numpy as jnp
        import numpy as np
        key = jax.random.key(seed)
        k0, k1, k2, k3 = jax.random.split(key, 4)
        B, S, D, F, E = (8, 256, 128, 256, 8)
        x = jax.random.normal(k0, (B, S, D), dtype=jnp.float32)
        Wg = jax.random.normal(k1, (D, E), dtype=jnp.float32) * 0.02
        W1 = jax.random.normal(k2, (E, D, F), dtype=jnp.float32) * 0.02
        W2 = jax.random.normal(k3, (E, F, D), dtype=jnp.float32) * 0.02
        return {'x': x, 'Wg': Wg, 'W1': W1, 'W2': W2}
    _L0_ffn_all = _L0_ffn_setup()
    _L0_ffn_in = {k: v for k, v in _L0_ffn_all.items() if k in ('Wg', 'W1', 'W2')}
    del _L0_ffn_all
    return {'x': x, 'ctx_1024': ctx_1024, 'mask_BxSxS2_ik1': mask_BxSxS2_ik1, 'L0_xattn_Wq': _L0_xattn_in['Wq'], 'L0_xattn_bq': _L0_xattn_in['bq'], 'L0_xattn_Wk': _L0_xattn_in['Wk'], 'L0_xattn_bk': _L0_xattn_in['bk'], 'L0_xattn_Wv': _L0_xattn_in['Wv'], 'L0_xattn_bv': _L0_xattn_in['bv'], 'L0_xattn_Wo': _L0_xattn_in['Wo'], 'L0_xattn_bo': _L0_xattn_in['bo'], 'L0_attn_w_q': _L0_attn_in['w_q'], 'L0_attn_w_k': _L0_attn_in['w_k'], 'L0_attn_w_v': _L0_attn_in['w_v'], 'L0_attn_w_o': _L0_attn_in['w_o'], 'L0_ffn_Wg': _L0_ffn_in['Wg'], 'L0_ffn_W1': _L0_ffn_in['W1'], 'L0_ffn_W2': _L0_ffn_in['W2']}

def reference(x, ctx_1024, mask_BxSxS2_ik1, L0_xattn_Wq, L0_xattn_bq, L0_xattn_Wk, L0_xattn_bk, L0_xattn_Wv, L0_xattn_bv, L0_xattn_Wo, L0_xattn_bo, L0_attn_w_q, L0_attn_w_k, L0_attn_w_v, L0_attn_w_o, L0_ffn_Wg, L0_ffn_W1, L0_ffn_W2):
    import jax
    import jax.numpy as jnp

    def _L0_xattn_ref(query, key, value, mask, Wq, bq, Wk, bk, Wv, bv, Wo, bo):
        import jax, jax.numpy as jnp
        import numpy as np
        HID = 128
        HEADS = 16
        HEAD_DIM = HID // HEADS

        def _split_heads(x, W, b):
            B, S, _ = x.shape
            y = x @ W + b
            return y.reshape(B, S, HEADS, HEAD_DIM).transpose(0, 2, 1, 3)
        B, S, _ = query.shape
        Q = _split_heads(query, Wq, bq)
        K = _split_heads(key, Wk, bk)
        V = _split_heads(value, Wv, bv)
        scale = 1.0 / jnp.sqrt(jnp.asarray(HEAD_DIM, dtype=Q.dtype))
        energy = jnp.einsum('bhqd,bhkd->bhqk', Q, K) * scale
        m = mask[:, None, :, :]
        energy = jnp.where(m == 0, jnp.asarray(-1000000000.0, dtype=energy.dtype), energy)
        attn = jax.nn.softmax(energy, axis=-1)
        out = jnp.einsum('bhqk,bhkd->bhqd', attn, V)
        out = out.transpose(0, 2, 1, 3).reshape(B, S, HID)
        return out @ Wo + bo

    def _L0_attn_ref(x, w_q, w_k, w_v, w_o):
        import jax, jax.numpy as jnp
        import numpy as np
        D_MODEL = 128
        N_HEAD = 16
        N_KV_HEAD = 4
        HEAD_DIM = D_MODEL // N_HEAD
        N_GROUP = N_HEAD // N_KV_HEAD
        ROPE_BASE = 10000.0
        ROPE_DIM = HEAD_DIM

        def _rope_tables(seq_len, dtype):
            half = ROPE_DIM // 2
            inv_freq = 1.0 / ROPE_BASE ** (jnp.arange(0, half, dtype=jnp.float32) * 2.0 / ROPE_DIM)
            pos = jnp.arange(seq_len, dtype=jnp.float32)
            freqs = pos[:, None] * inv_freq[None, :]
            return (jnp.cos(freqs).astype(dtype), jnp.sin(freqs).astype(dtype))

        def _apply_rope(t):
            S = t.shape[2]
            cos, sin = _rope_tables(S, t.dtype)
            half = ROPE_DIM // 2
            t1 = t[..., :half]
            t2 = t[..., half:ROPE_DIM]
            rot = jnp.concatenate([t1 * cos - t2 * sin, t1 * sin + t2 * cos], axis=-1)
            if ROPE_DIM < t.shape[-1]:
                rot = jnp.concatenate([rot, t[..., ROPE_DIM:]], axis=-1)
            return rot
        B, S, _ = x.shape
        q = (x @ w_q).reshape(B, S, N_HEAD, HEAD_DIM).transpose(0, 2, 1, 3)
        k = (x @ w_k).reshape(B, S, N_KV_HEAD, HEAD_DIM).transpose(0, 2, 1, 3)
        v = (x @ w_v).reshape(B, S, N_KV_HEAD, HEAD_DIM).transpose(0, 2, 1, 3)
        q = _apply_rope(q)
        k = _apply_rope(k)
        k = jnp.repeat(k, N_GROUP, axis=1)
        v = jnp.repeat(v, N_GROUP, axis=1)
        scale = 1.0 / jnp.sqrt(jnp.asarray(HEAD_DIM, dtype=x.dtype))
        scores = jnp.einsum('bhqd,bhkd->bhqk', q, k) * scale
        attn = jax.nn.softmax(scores, axis=-1)
        out = jnp.einsum('bhqk,bhkd->bhqd', attn, v)
        out = out.transpose(0, 2, 1, 3).reshape(B, S, D_MODEL)
        return out @ w_o

    def _L0_ffn_ref(x, Wg, W1, W2):
        import jax, jax.numpy as jnp
        import numpy as np
        B, S, D = x.shape
        E = Wg.shape[1]
        T = B * S
        cap = max(1, T // E)
        xt = x.reshape(T, D)
        logits = xt @ Wg
        probs = jax.nn.softmax(logits, axis=-1)
        pT = probs.T
        _, top_idx = jax.lax.top_k(pT, cap)
        sel = jnp.zeros((E, T), dtype=bool).at[jnp.arange(E)[:, None], top_idx].set(True)
        masked = jnp.where(sel, pT, -jnp.inf)
        assigned = sel.any(axis=0)
        tok2exp = jnp.where(assigned, jnp.argmax(masked, axis=0), jnp.argmax(pT, axis=0))
        weights = jnp.take_along_axis(probs, tok2exp[:, None], axis=1)[:, 0]
        out = jnp.zeros_like(xt)
        for e in range(E):
            gate = jnp.where(tok2exp == e, weights, 0.0)
            h = jax.nn.gelu(xt @ W1[e], approximate=False) @ W2[e]
            out = out + gate[:, None] * h
        return out.reshape(B, S, D)
    x = x + _L0_xattn_ref(_layernorm(x, axis=-1), ctx_1024, ctx_1024, mask_BxSxS2_ik1, L0_xattn_Wq, L0_xattn_bq, L0_xattn_Wk, L0_xattn_bk, L0_xattn_Wv, L0_xattn_bv, L0_xattn_Wo, L0_xattn_bo)
    x = x + _L0_attn_ref(_layernorm(x, axis=-1), L0_attn_w_q, L0_attn_w_k, L0_attn_w_v, L0_attn_w_o)
    x = x + _L0_ffn_ref(_layernorm(x, axis=-1), L0_ffn_Wg, L0_ffn_W1, L0_ffn_W2)
    return x

_drawn_inputs = setup_inputs


def setup_inputs(seed=0):
    import zlib

    import numpy as np

    out = dict(_drawn_inputs(seed))
    spreads = {'L0_xattn_bq': (0.0, 0.307),
     'L0_xattn_bk': (0.0, 0.8),
     'L0_xattn_bv': (0.0, 0.1),
     'L0_xattn_bo': (0.0, 0.1)}
    factors = {'L0_ffn_Wg': 8.0, 'L0_ffn_W1': 8.0, 'L0_ffn_W2': 8.0}
    for name, (base, spread) in spreads.items():
        noise = np.random.default_rng([zlib.crc32(name.encode()), seed]).standard_normal(out[name].shape)
        drawn = base * np.exp(spread * noise) if base else spread * noise
        out[name] = jnp.asarray(drawn.astype(out[name].dtype))
    for name, factor in factors.items():
        out[name] = (out[name] * factor).astype(out[name].dtype)
    return out
```

```python
from contextlib import ExitStack

import numpy as np

import concourse.bass as bass
from concourse import mybir

F32 = mybir.dt.float32
I32 = mybir.dt.int32
ALU = mybir.AluOpType
ACT = mybir.ActivationFunctionType
AX_X = mybir.AxisListType.X

P = 128
HD = 8
NG = 4
SQ = 32
BT = P // SQ
BIG = float(2.0 ** 100)
EPS = 1e-5


def shape_constants(B, S):
    c = np.arange(P)
    one = np.float32
    out = {}
    out["ident"] = np.eye(P, dtype=one)
    out["headmask"] = (((c % 32) // HD)[:, None] == np.arange(4)[None, :]).astype(one)
    out["ownhead"] = ((c // HD)[:, None] == np.arange(16)[None, :]).astype(one)
    out["groupmask"] = (np.arange(4)[:, None] == (c // 32)[None, :]).astype(one)
    out["quadmask"] = ((c // 32)[:, None] == np.arange(4)[None, :]).astype(one)
    f = (c % HD) % 4
    inv = (1.0 / np.float32(10000.0) ** (np.arange(4, dtype=one) * 2.0 / HD)).astype(one)
    ang = (np.arange(S, dtype=one)[None, :] * inv[f][:, None]).astype(one)
    sign = np.where(c % HD < 4, -1.0, 1.0).astype(one)[:, None]
    out["rope"] = np.concatenate([np.cos(ang), np.sin(ang) * sign], axis=1).astype(one)
    e, t = c % 8, c // 8
    same = e[:, None] == e[None, :]
    out["same_expert"] = same.astype(one)
    out["earlier_tile"] = (same & (t[:, None] < t[None, :])).astype(one)
    out["rank"] = np.broadcast_to(8.0 - np.arange(8), (P, 8)).astype(one).copy()
    return out


_CONSTS = ["ident", "headmask", "ownhead", "groupmask", "quadmask", "rope", "same_expert", "earlier_tile", "rank"]


def perceiver_block(nc, x, ctx_in, mask, Wq, bq, Wk, bk, Wv, bv, Wo, bo,
                    w_q, w_k, w_v, w_o, Wg, W1, W2,
                    c_ident, c_head, c_own, c_group, c_quad, c_rope, c_same, c_earlier, c_rank, out):
    NB, S, D = x.shape
    S2 = ctx_in.shape[1]
    T = NB * S
    NT = T // P
    KC = (S2 - 1) // P
    E, F = Wg.shape[1], W1.shape[2]
    FC = F // P
    CAP = max(1, T // E)
    assert (D, S, NB % BT, S2 - KC * P, E) == (P, SQ, 0, 1, 8)
    SCALE = 1.0 / float(np.sqrt(np.float32(HD)))
    HALVES = NT // 16

    with ExitStack() as ctx:
        def sb(name, shape, dt=F32):
            return ctx.enter_context(nc.sbuf_tensor(name, shape, dt))

        def sem(name):
            return ctx.enter_context(nc.semaphore(name))

        psum = [ctx.enter_context(nc.psum_tensor(f"bank{i}", [P, 512], F32)) for i in range(8)]

        ident = sb("ident", [P, P])
        headmask = sb("headmask", [P, 4])
        ownhead = sb("ownhead", [P, 16])
        groupmask = sb("groupmask", [4, P])
        quadmask = sb("quadmask", [P, 4])
        rope = sb("rope", [P, 2, S])
        same = sb("same", [P, P])
        earlier = sb("earlier", [P, P])
        rank = sb("rank", [P, 8])
        wq_s = sb("wq_s", [P, P])
        wk_s = sb("wk_s", [P, P])
        wv_s = sb("wv_s", [P, P])
        wo_s = sb("wo_s", [P, P])
        bias = sb("bias", [P, 3])
        bo_s = sb("bo_s", [1, P])
        brow = sb("brow", [1, P])
        ones1 = sb("ones1", [1, P])
        sw_q = sb("sw_q", [P, P])
        sw_k = sb("sw_k", [P, NG * HD])
        sw_v = sb("sw_v", [P, NG * HD])
        sw_o = sb("sw_o", [P, P])
        wqk = sb("wqk", [P, 4, P])
        wg_s = sb("wg_s", [P, E])
        w1_s = sb("w1_s", [P, E, F])
        w2_s = sb("w2_s", [P, E, FC, P])

        X = sb("X", [P, NT, P])
        QT = sb("QT", [P, T])
        OT = sb("OT", [P, T])
        XTT = QT
        stats = sb("stats", [P, NT, 6])
        mv = sb("mv", [P, NT, 2])
        std = sb("std", [P, NT])
        rstd = sb("rstd", [P, NT])
        RSUM = sb("RSUM", [P, NT, BT, NG])
        RIN = sb("RIN", [P, 4, NT, NG])

        xn = sb("xn", [P, 4, P])
        xg = sb("xg", [P, 2, 512])

        CX = sb("CX", [P, BT, KC, P])
        CXE = sb("CXE", [1, BT, P])
        MK = sb("MK", [P, BT, S2], I32)
        MB = sb("MB", [P, 2, S2])
        CT = sb("CT", [P, 2, S2])
        KT = sb("KT", [P, 2, S2])
        VT = sb("VT", [P, BT, KC * P])
        VE = sb("VE", [4, BT, P])
        QB = sb("QB", [P, 2, NG * 4, SQ])
        SM = sb("SM", [P, NG, S2])
        MN = sb("MN", [P, NG])
        PR = sb("PR", [P, 2, NG, S2])
        PT = sb("PT", [P, 2, KC * P])
        PTE = sb("PTE", [4, 2, P])
        OM = sb("OM", [P, 2, 4, SQ])

        RIE = sb("RIE", [P, 2, P])
        OTN = sb("OTN", [P, 2, P])

        xt = sb("xt", [P, 4, P])
        TQ = sb("TQ", [P, 4, 4, P])
        QKR = sb("QKR", [P, 4, 2, P])
        KB = sb("KB", [P, 4, BT, NG, SQ])
        VB = sb("VB", [P, 4, BT, NG, HD])
        SX = sb("SX", [P, 4, 16, SQ])
        smx = sb("smx", [P, 4, 16])
        ssum = sb("ssum", [P, 4, 16])
        sinv = sb("sinv", [P, 4, 16])
        SP = sb("SP", [P, 4, BT, P])
        SO = sb("SO", [P, 4, P])

        PRB = sb("PRB", [P, NT, E])
        rmx = sb("rmx", [P, NT])
        PRT = sb("PRT", [P, HALVES, P])
        cmp_ = sb("cmp", [P, HALVES, P])
        cnt = sb("cnt", [P, 1])
        thr = sb("thr", [P, 1], I32)
        thr_try = sb("thr_try", [P, 1], I32)
        bit_ok = sb("bit_ok", [P, 1], I32)
        GT = sb("GT", [P, HALVES, P])
        EQ = sb("EQ", [P, HALVES, P])
        PFX = sb("PFX", [P, HALVES, P])
        tot = sb("tot", [P, 2])
        need = sb("need", [P, 2])
        SEL = sb("SEL", [P, NT, E])
        KEY = sb("KEY", [P, NT, E])
        RT = sb("RT", [P, NT, E])
        any_ = sb("any_", [P, NT])
        GATE = sb("GATE", [P, NT, E])
        HT = sb("HT", [P, 2, FC, 512])
        zero_row = sb("zero_row", [P, P])
        warm = sb("warm", [1, 1])
        waited = sb("waited", [1, NG])

        ld_x = sem("ld_x")
        ld_w = sem("ld_w")
        ld_ffn = sem("ld_ffn")
        dve_c = sem("dve_c")
        n0_std = sem("n0_std")
        n0_rstd = sem("n0_rstd")
        n0_xn = sem("n0_xn")
        n0_tr = sem("n0_tr")
        n0_xt = sem("n0_xt")
        n0_q = sem("n0_q")
        n0_qt = sem("n0_qt")
        warm_ok = sem("warm_ok")
        NLX = 4

        ld_ctx = [sem(f"ld_ctx{b}") for b in range(BT)]
        ld_mask = [sem(f"ld_mask{b}") for b in range(BT)]
        pe_l = sem("pe_l")
        pe_k = sem("pe_k")
        pe_v = sem("pe_v")
        pe_s = sem("pe_s")
        pe_t = sem("pe_t")
        pe_a = sem("pe_a")
        ev_l = sem("ev_l")
        ev_k = sem("ev_k")
        ev_v = sem("ev_v")
        ev_t = sem("ev_t")
        ev_o = sem("ev_o")
        dve_om = sem("dve_om")
        dve_min = sem("dve_min")
        act_exp = sem("act_exp")
        pool_q = sem("pool_q")
        pool_m = sem("pool_m")

        pe_rs = sem("pe_rs")
        dve_rs = sem("dve_rs")
        pool_r = sem("pool_r")
        pe_r = sem("pe_r")
        dve_otn = sem("dve_otn")
        pe_x1 = sem("pe_x1")
        dve_x1 = sem("dve_x1")
        dve_st1 = sem("dve_st1")
        brow_pe = sem("brow_pe")
        brow_ok = sem("brow_ok")
        n1_std = sem("n1_std")
        n1_rstd = sem("n1_rstd")

        a_xn = sem("a_xn")
        a_tr = sem("a_tr")
        a_xt = sem("a_xt")
        a_pj = sem("a_pj")
        a_tq = sem("a_tq")
        a_qk = sem("a_qk")
        a_vb = sem("a_vb")
        a_kb = sem("a_kb")
        a_s = sem("a_s")
        a_mx = sem("a_mx")
        a_sx = sem("a_sx")
        a_ex = sem("a_ex")
        a_sum = sem("a_sum")
        a_inv = sem("a_inv")
        a_pn = sem("a_pn")
        a_pt = sem("a_pt")
        a_sp = sem("a_sp")
        a_o = sem("a_o")
        a_so = sem("a_so")
        a_wo = sem("a_wo")
        a_x2 = sem("a_x2")
        a_st = sem("a_st")
        wqk_ok = sem("wqk_ok")
        n2_std = sem("n2_std")
        n2_rstd = sem("n2_rstd")

        r_xn = sem("r_xn")
        r_tr = sem("r_tr")
        r_xt = sem("r_xt")
        r_xtt = sem("r_xtt")
        r_lg = sem("r_lg")
        r_cp = sem("r_cp")
        t_act = sem("t_act")
        t_exp = sem("t_exp")
        t_pe = sem("t_pe")
        t_dve = sem("t_dve")
        t_done = sem("t_done")
        f_h = sem("f_h")
        f_g = sem("f_g")
        f_y = sem("f_y")
        f_x = sem("f_x")
        st_out = sem("st_out")

        block = ctx.enter_context(nc.Block())

        x_tiles = x.rearrange("(i b) s d -> (b s) i d", b=BT)
        out_tiles = out.rearrange("(i b) s d -> (b s) i d", b=BT)
        bits = list(range(29, -1, -1))

        def wait_reuse(eng, s, v):
            if not (isinstance(v, int) and v <= 0):
                eng.wait_ge(s, v)

        def peeled(eng, n, body):
            body(0)
            with eng.Fori(1, n) as i:
                body(i)

        def mm(o, l, r, start=True, stop=True):
            return nc.tensor.matmul(o, l, r, start=start, stop=stop, skip_group_check=True)

        def tr(o, i, n=P):
            return nc.tensor.transpose(o, i, ident[0:n, 0:n])

        small = [(wq_s, Wq), (wk_s, Wk), (wv_s, Wv), (wo_s, Wo), (ident, c_ident), (headmask, c_head), (ownhead, c_own),
                 (groupmask, c_group), (quadmask, c_quad), (same, c_same), (earlier, c_earlier),
                 (rank, c_rank), (sw_q, w_q), (sw_k, w_k), (sw_v, w_v), (wg_s, Wg)]
        NW = 16 * (len(small) + 6 + 3 + 1)

        @block.sync
        def _(sp):
            for j in range(NLX):
                n = NT // NLX
                sp.dma_start(X[:, j * n:(j + 1) * n, :], x_tiles[:, j * n:(j + 1) * n, :]).then_inc(ld_x, 16)

            def load_batch(i, b, first):
                if not first:
                    sp.wait_ge(pe_l, i * BT + (b - BT + 1))
                sp.dma_start(CX[:, b, :, :], ctx_in[bass.ds(i * BT + b, 1), 0:KC * P, :]
                             .rearrange("a (j p) c -> p (a j) c", p=P)).then_inc(ld_ctx[b], 16)
                sp.dma_start(CXE[0:1, b, :], ctx_in[bass.ds(i * BT + b, 1), KC * P, :]).then_inc(ld_ctx[b], 16)
                if not first:
                    sp.wait_ge(pool_m, i * BT + (b - BT + 1))
                for r in range(4):
                    sp.dma_start(MK[r * SQ:(r + 1) * SQ, b, :],
                                 mask[bass.ds(i * BT + b, 1), :, :].rearrange("a q k -> (a q) k"))\
                        .then_inc(ld_mask[b], 16)

            for b in range(BT):
                load_batch(0, b, True)
            with sp.Fori(1, NT) as i:
                for b in range(BT):
                    load_batch(i, b, False)
            sp.dma_start(w1_s[:, :, :], W1.rearrange("e c f -> c e f")).then_inc(ld_ffn, 16)
            sp.dma_start(w2_s[:, :, :, :], W2.rearrange("e (j f) c -> f e j c", f=P)).then_inc(ld_ffn, 16)
            with sp.Fori(0, NT // 4) as g:
                sp.wait_ge(f_x, (g + 1) * (4 * E))
                sp.dma_start(out_tiles[:, bass.ds(g * 4, 4), :], X[:, bass.ds(g * 4, 4), :]).then_inc(st_out, 16)
            sp.wait_ge(st_out, 16 * (NT // 4))

        @block.scalar
        def _(act):
            for dst, src in small:
                act.dma_start(dst[:, :], src).then_inc(ld_w, 16)
            for j, bvec in enumerate((bq, bk, bv)):
                act.dma_start(bias[:, j:j + 1], bvec.rearrange("(c a) -> c a", a=1)).then_inc(ld_w, 16)
            act.dma_start(bo_s[:, :], bo.rearrange("(a c) -> a c", a=1)).then_inc(ld_w, 16)
            act.dma_start(rope[:, :, :], c_rope.rearrange("p (a s) -> p a s", a=2)).then_inc(ld_w, 16)
            for g in range(NG):
                act.dma_start(sw_o[g * 32:(g + 1) * 32, :],
                              w_o.rearrange("(k g d) c -> g k d c", k=NG, g=4)[g]).then_inc(ld_w, 16)
            act.dma_start(brow[:, :], bo.rearrange("(a c) -> a c", a=1)).then_inc(ld_w, 16)

            act.wait_ge(warm_ok, 1)
            act.wait_ge(n0_std, 1)
            nc.scalar.activation(std[:, :], std[:, :], ACT.Sqrt).then_inc(n0_rstd, 1)
            with act.Fori(0, NT // 8) as i:
                for h in range(2):
                    act.wait_ge(n0_tr, i * 2 + (h + 1))
                    nc.scalar.activation(xg[:, h, :], psum[h][:, :], ACT.Copy).then_inc(n0_xt, 1)

            def evac_ctx(n, b):
                act.wait_ge(pe_l, n + 1)
                nc.scalar.activation(CT[:, b % 2, :], psum[0][:, 0:S2], ACT.Copy).then_inc(ev_l, 1)

            def evac_k(n, b):
                act.wait_ge(pe_k, n + 1)
                nc.scalar.activation(KT[:, b % 2, :], psum[1][:, 0:S2], ACT.Identity,
                                     bias=bias[:, 1:2]).then_inc(ev_k, 1)

            def exp_group(n, i, b, g):
                act.wait_ge(dve_min, 4 * n + (g + 1))
                nc.scalar.activation(PR[:, b % 2, g, :], SM[:, g, :], ACT.Exp, bias=MN[:, g:g + 1], scale=-1.0,
                                     accum_out=RSUM[:, bass.ds(i, 1), b, g:g + 1].rearrange("p a g -> p (a g)"))\
                    .then_inc(act_exp, 1)

            def batch(i, b, more):
                n = i * BT + b
                exp_group(n, i, b, 0)
                if more:
                    evac_ctx(n + 1, b + 1)
                exp_group(n, i, b, 1)
                if more:
                    evac_k(n + 1, b + 1)
                exp_group(n, i, b, 2)
                exp_group(n, i, b, 3)

            nc.scalar.activation(warm[:, :], warm[:, :], ACT.Exp)
            evac_ctx(0, 0)
            evac_k(0, 0)
            with act.Fori(0, NT - 1) as i:
                for b in range(BT):
                    batch(i, b, True)
            for b in range(BT):
                batch(NT - 1, b, b < BT - 1)

            act.wait_ge(n1_std, 1)
            nc.scalar.activation(std[:, :], std[:, :], ACT.Sqrt).then_inc(n1_rstd, 1)

            nc.scalar.activation(warm[:, :], warm[:, :], ACT.Exp)
            with act.Fori(0, NT // 4) as i:
                for j in range(4):
                    act.wait_ge(a_tr, i * 4 + (j + 1))
                    nc.scalar.activation(xt[:, j, :], psum[j][:, 0:P], ACT.Copy).then_inc(a_xt, 1)
                for j in range(4):
                    act.wait_ge(a_sx, i * 4 + (j + 1))
                    nc.scalar.activation(SX[:, j, :, :], SX[:, j, :, :], ACT.Exp, scale=SCALE).then_inc(a_ex, 1)
                for j in range(4):
                    act.wait_ge(a_pt, i * 4 + (j + 1))
                    nc.scalar.activation(SP[:, j, :, :].rearrange("p b k -> p (b k)"), psum[4 + j][:, :],
                                         ACT.Copy).then_inc(a_sp, 1)
                for j in range(4):
                    act.wait_ge(a_o, i * 4 + (j + 1))
                    nc.scalar.activation(SO[:, j, :], psum[j][:, 0:P], ACT.Copy).then_inc(a_so, 1)

            act.wait_ge(n2_std, 1)
            nc.scalar.activation(std[:, :], std[:, :], ACT.Sqrt).then_inc(n2_rstd, 1)
            with act.Fori(0, NT // 8) as i:
                for h in range(2):
                    act.wait_ge(r_tr, i * 2 + (h + 1))
                    nc.scalar.activation(xg[:, h, :], psum[h][:, :], ACT.Copy).then_inc(r_xt, 1)
            act.wait_ge(t_act, 1)
            nc.scalar.activation(PRB[:, :, :], PRB[:, :, :], ACT.Exp).then_inc(t_exp, 1)

            nc.scalar.activation(warm[:, :], warm[:, :], ACT.Gelu)
            with act.Fori(0, NT // 4) as i:
                for e in range(E):
                    for j in range(FC):
                        act.wait_ge(f_h, i * (E * FC) + (e * FC + j + 1))
                        if j == 0 and e >= 2:
                            act.wait_ge(f_y, i * E + (e - 1))
                        nc.scalar.activation(HT[:, e % 2, j, :], psum[2 * (e % 2) + j][:, :], ACT.Gelu)\
                            .then_inc(f_g, 1)

        @block.gpsimd
        def _(pool):
            nc.gpsimd.memset(warm[:, :], 0.0).then_inc(warm_ok, 1)
            nc.gpsimd.memset(ones1[:, :], 1.0)
            nc.gpsimd.memset(zero_row[:, :], 0.0)

            pool.wait_ge(ld_w, NW)
            pool.wait_ge(n0_qt, NT // 4)

            def batch(i, b, first):
                n = i * BT + b
                if not first:
                    pool.wait_ge(pe_s, 4 * n - 4)
                    pool.wait_ge(dve_min, 4 * n - 4)
                pool.wait_ge(ld_mask[b], 64 * i + 64)
                nc.gpsimd.tensor_tensor(
                    QB[:, b % 2, :, :],
                    QT[:, bass.ds(n * SQ, SQ)].rearrange("p (a q) -> p a q", a=1).broadcast_to([P, 16, SQ]),
                    ownhead[:, :].rearrange("p (a h) -> p h a", a=1).broadcast_to([P, 16, SQ]),
                    ALU.mult).then_inc(pool_q, 1)
                nc.gpsimd.tensor_scalar(MB[:, b % 2, :], MK[:, b, :], 0.0, BIG, ALU.is_equal, ALU.mult)\
                    .then_inc(pool_m, 1)

            for b in range(BT):
                batch(0, b, b < 2)
            with pool.Fori(1, NT) as i:
                for b in range(BT):
                    batch(i, b, False)

            pool.wait_ge(dve_rs, 1)
            def spread(i):
                for h in range(2):
                    wait_reuse(pool, pe_r, i * 2)
                    nc.gpsimd.tensor_copy(
                        RIE[:, h, :].rearrange("p (g k d) -> p g k d", g=NG, k=4),
                        RIN[:, :, bass.ds(i * 2 + h, 1), :].rearrange("p k a g -> p g k a")
                        .broadcast_to([P, NG, 4, HD])).then_inc(pool_r, 1)

            peeled(pool, NT // 2, spread)

            with pool.Fori(0, NT // 4) as i:
                for j in range(4):
                    pool.wait_ge(a_qk, i * 4 + (j + 1))
                    for b in range(BT):
                        ins = nc.gpsimd.tensor_tensor(
                            KB[:, j, b, :, :],
                            QKR[:, j, 1, b * SQ:(b + 1) * SQ].rearrange("p (a q) -> p a q", a=1)
                            .broadcast_to([P, NG, SQ]),
                            headmask[:, :].rearrange("p (a h) -> p h a", a=1).broadcast_to([P, NG, SQ]),
                            ALU.mult)
                    ins.then_inc(a_kb, 1)
                for j in range(4):
                    pool.wait_ge(a_inv, i * 4 + (j + 1))
                    nc.gpsimd.tensor_tensor(
                        SX[:, j, :, :], SX[:, j, :, :],
                        sinv[:, j, :].rearrange("p (n a) -> p n a", a=1).broadcast_to([P, 16, SQ]),
                        ALU.mult).then_inc(a_pn, 1)

            with pool.Fori(0, NT // 8) as i:
                for h in range(2):
                    pool.wait_ge(r_xt, i * 2 + (h + 1))
                    nc.gpsimd.tensor_copy(XTT[:, bass.ds((i * 2 + h) * 512, 512)], xg[:, h, :])\
                        .then_inc(r_xtt, 1)

        @block.tensor
        def _(pe):
            pe.wait_ge(ld_w, NW)
            def queries(i):
                for h in range(2):
                    for j in range(4):
                        pe.wait_ge(n0_xn, i * 8 + (h * 4 + j + 1))
                        last = tr(psum[h][:, j * P:(j + 1) * P], xn[:, j, :])
                    last.then_inc(n0_tr, 1)
                    pe.wait_ge(n0_xt, i * 2 + (h + 1))
                    wait_reuse(pe, n0_qt, i * 2 + h)
                    mm(psum[2 + h][:, :], wq_s[:, :], xg[:, h, :]).then_inc(n0_q, 1)

            peeled(pe, NT // 8, queries)

            def ctx_transpose(n, i, b, first):
                pe.wait_ge(ld_ctx[b % BT], 32 * i + 32)
                if not first:
                    pe.wait_ge(ev_v, n)
                for j in range(KC):
                    tr(psum[0][:, j * P:(j + 1) * P], CX[:, b % BT, j, :])
                tr(psum[0][:, KC * P:S2], CXE[0:1, b % BT, :], 1).then_inc(pe_l, 1)

            def keys(n, b, first):
                pe.wait_ge(ev_l, n + 1)
                if not first:
                    pe.wait_ge(ev_k, n)
                mm(psum[1][:, 0:S2], wk_s[:, :], CT[:, b % 2, :]).then_inc(pe_k, 1)

            def values(n, b):
                pe.wait_ge(ev_l, n + 1)
                for j in range(KC):
                    mm(psum[0][:, j * P:(j + 1) * P], CT[:, b % 2, j * P:(j + 1) * P], wv_s[:, :])
                mm(psum[0][0:4, KC * P:KC * P + P], CT[:, b % 2, KC * P:S2].broadcast_to([P, 4]), wv_s[:, :])\
                    .then_inc(pe_v, 1)

            def energy(n, b, g, first):
                if g == 0:
                    pe.wait_ge(ev_k, n + 1)
                    pe.wait_ge(pool_q, n + 1)
                if not (first and g < 2):
                    pe.wait_ge(dve_min, 4 * n + (g - 1))
                mm(psum[2 + g % 2][:, 0:S2], QB[:, b % 2, 4 * g:4 * g + 4, :].rearrange("p h q -> p (h q)"),
                   KT[:, b % 2, :]).then_inc(pe_s, 1)

            def turn(m, b, g, first):
                if g == 0:
                    pe.wait_ge(act_exp, 4 * m + 4)
                if not (first and g < 2):
                    pe.wait_ge(ev_t, 4 * m + (g - 1))
                bank = psum[4 + g % 2]
                if g == 0:
                    tr(bank[0:4, KC * P:KC * P + P], PR[:, b % 2, :, KC * P])
                for j in range(KC):
                    last = tr(bank[:, j * P:(j + 1) * P], PR[:, b % 2, g, j * P:(j + 1) * P])
                last.then_inc(pe_t, 1)

            def attend_last_key(m, q, b, first):
                pe.wait_ge(ev_t, 4 * m + 1)
                pe.wait_ge(ev_v, m + 1)
                if b % 2 == 0 and not first:
                    pe.wait_ge(ev_o, q - 1)
                col = (b % 2) * P
                mm(psum[6 + b // 2][:, col:col + P], VE[:, b, :], PTE[:, b % 2, :], start=True, stop=False)

            def attend(m, b, g):
                pe.wait_ge(ev_t, 4 * m + (g + 1))
                col = (b % 2) * P
                for j in range(KC):
                    last = mm(psum[6 + b // 2][32 * g:32 * g + 32, col:col + P],
                              VT[:, b, j * P + 32 * g:j * P + 32 * g + 32],
                              PT[:, g % 2, j * P:(j + 1) * P], start=False, stop=(j == KC - 1))
                last.then_inc(pe_a, 1)

            def step(i, b, prev, more, first_tile, second_tile_start):
                n = i * BT + b
                pb = (b - 1) % BT
                pq = (i * BT + b - 1) if False else None
                m = n - 1
                pair = i * 2 + (b - 1) // 2 if b >= 1 else i * 2 - 1
                o_new = first_tile and b >= 1
                nb, ni = (b + 1) % BT, i + (b + 1) // BT
                energy(n, b, 0, first_tile and b == 0)
                if prev:
                    turn(m, pb, 0, first_tile and b == 1)
                if more:
                    ctx_transpose(n + 1, ni, nb, False)
                energy(n, b, 1, first_tile and b == 0)
                if prev:
                    turn(m, pb, 1, first_tile and b == 1)
                    attend_last_key(m, pair, pb, o_new)
                    attend(m, pb, 0)
                if more:
                    keys(n + 1, nb, False)
                energy(n, b, 2, False)
                if prev:
                    turn(m, pb, 2, False)
                    attend(m, pb, 1)
                energy(n, b, 3, False)
                if prev:
                    turn(m, pb, 3, False)
                    attend(m, pb, 2)
                if more:
                    values(n + 1, nb)
                if prev:
                    attend(m, pb, 3)

            pe.wait_ge(n0_qt, NT // 4)
            ctx_transpose(0, 0, 0, True)
            keys(0, 0, True)
            values(0, 0)
            for b in range(BT):
                step(0, b, b > 0, True, True, False)
            with pe.Fori(1, NT - 1) as i:
                for b in range(BT):
                    step(i, b, True, True, False, False)
            for b in range(BT):
                step(NT - 1, b, True, b < BT - 1, False, False)
            m = NB - 1
            for g in range(NG):
                turn(m, BT - 1, g, False)
                if g == 0:
                    attend_last_key(m, m // 2, BT - 1, False)
                attend(m, BT - 1, g)

            pe.wait_ge(ev_t, 4 * NB)
            pe.wait_ge(act_exp, 4 * NB)
            for k in range(4):
                for b in range(BT):
                    last = mm(psum[k][32 * b:32 * b + 32, 0:NT * NG],
                              ident[32 * k:32 * k + 32, 32 * k:32 * k + 32],
                              RSUM[32 * k:32 * k + 32, :, b, :])
            last.then_inc(pe_rs, 1)
            mm(psum[4][0:1, 0:P], bias[:, 2:3], wo_s[:, :]).then_inc(brow_pe, 1)
            pe.wait_ge(brow_ok, 1)
            pe.wait_ge(dve_rs, 1)
            pe.wait_ge(ev_o, NB // 2)
            with pe.Fori(0, NT // 2) as i:
                for h in range(2):
                    pe.wait_ge(pool_r, i * 2 + (h + 1))
                    tr(psum[h][:, 0:P], RIE[:, h, :]).then_inc(pe_r, 1)
                for h in range(2):
                    pe.wait_ge(dve_otn, i * 2 + (h + 1))
                    mm(psum[2 + h][:, 0:P], OTN[:, h, :], wo_s[:, :], start=True, stop=False)
                    mm(psum[2 + h][:, 0:P], ones1[0:1, :], brow[0:1, :], start=False, stop=True)\
                        .then_inc(pe_x1, 1)

            pe.wait_ge(wqk_ok, 1)
            pe.wait_ge(dve_x1, NT)
            with pe.Fori(0, NT // 4) as i:
                for j in range(4):
                    pe.wait_ge(a_xn, i * 4 + (j + 1))
                    tr(psum[j][:, 0:P], xn[:, j, :]).then_inc(a_tr, 1)
                for j in range(4):
                    pe.wait_ge(a_xt, i * 4 + (j + 1))
                    for w in range(4):
                        mm(psum[4 + j][:, w * P:(w + 1) * P], wqk[:, w, :], xt[:, j, :])
                    for b in range(BT):
                        for g in range(4):
                            last = mm(psum[j][32 * g:32 * g + 32, P + 32 * b:P + 32 * b + 32],
                                      xt[:, j, b * SQ:(b + 1) * SQ], sw_v[:, :])
                    last.then_inc(a_pj, 1)
                for j in range(4):
                    pe.wait_ge(dve_x1, NT)
                    pe.wait_ge(a_vb, i * 4 + (j + 1))
                    pe.wait_ge(a_kb, i * 4 + (j + 1))
                    for b in range(BT):
                        for g in range(4):
                            rows = slice(32 * g, 32 * g + 32)
                            last = mm(psum[j][rows, b * P:(b + 1) * P],
                                      QKR[rows, j, 0, b * SQ:(b + 1) * SQ],
                                      KB[rows, j, b, :, :].rearrange("p h q -> p (h q)"))
                    last.then_inc(a_s, 1)
                for j in range(4):
                    pe.wait_ge(a_pn, i * 4 + (j + 1))
                    for b in range(BT):
                        last = tr(psum[4 + j][:, b * P:(b + 1) * P],
                                  SX[:, j, 4 * b:4 * b + 4, :].rearrange("p n k -> p (n k)"))
                    last.then_inc(a_pt, 1)
                for j in range(4):
                    pe.wait_ge(a_sp, i * 4 + (j + 1))
                    for b in range(BT):
                        for g in range(4):
                            last = mm(psum[j][32 * g:32 * g + 32, b * SQ:(b + 1) * SQ],
                                      VB[:, j, b, :, :].rearrange("p h d -> p (h d)"),
                                      SP[:, j, b, g * SQ:(g + 1) * SQ])
                    last.then_inc(a_o, 1)
                for j in range(4):
                    pe.wait_ge(a_so, i * 4 + (j + 1))
                    mm(psum[4 + j][:, 0:P], SO[:, j, :], sw_o[:, :]).then_inc(a_wo, 1)

            pe.wait_ge(a_x2, NT)
            def route(i):
                for h in range(2):
                    wait_reuse(pe, r_xtt, i * 2 + h)
                    for j in range(4):
                        pe.wait_ge(r_xn, i * 8 + (h * 4 + j + 1))
                        last = tr(psum[h][:, j * P:(j + 1) * P], xn[:, j, :])
                    last.then_inc(r_tr, 1)
                    pe.wait_ge(r_xt, i * 2 + (h + 1))
                    wait_reuse(pe, r_cp, i * 2 + h)
                    for j in range(4):
                        last = mm(psum[2 + h][:, j * E:(j + 1) * E], xg[:, h, j * P:(j + 1) * P], wg_s[:, :])
                    last.then_inc(r_lg, 1)

            peeled(pe, NT // 8, route)

            pe.wait_ge(t_dve, 1)
            for a in range(HALVES):
                last = tr(psum[0][:, a * P:(a + 1) * P],
                          PRB[:, a * 16:(a + 1) * 16, :].rearrange("p i e -> p (i e)"))
            last.then_inc(t_pe, 1)
            for k in range(len(bits)):
                pe.wait_ge(t_dve, 2 + k)
                mm(psum[1][:, 0:1], same[:, :], cnt[:, :]).then_inc(t_pe, 1)
            nb = len(bits)
            pe.wait_ge(t_dve, 2 + nb)
            mm(psum[2][:, 0:1], same[:, :], cnt[:, :]).then_inc(t_pe, 1)
            pe.wait_ge(t_dve, 3 + nb)
            for a in range(HALVES):
                for c in range(a + 1):
                    last = mm(psum[3][:, a:a + 1], earlier[:, :] if c == a else same[:, :], tot[:, c:c + 1],
                              start=(c == 0), stop=(c == a))
            last.then_inc(t_pe, 1)
            pe.wait_ge(t_dve, 4 + nb)
            for a in range(HALVES):
                last = tr(psum[0][:, a * P:(a + 1) * P], GT[:, a, :])
            last.then_inc(t_pe, 1)

            pe.wait_ge(ld_ffn, 32)
            pe.wait_ge(r_xtt, NT // 4)
            pe.wait_ge(t_done, 1)

            def hidden(i, e, wait):
                for j in range(FC):
                    if wait:
                        pe.wait_ge(f_g, i * (E * FC) + ((e - 2) * FC + j + 1))
                    mm(psum[2 * (e % 2) + j][:, :], w1_s[:, e, j * P:(j + 1) * P],
                       XTT[:, bass.ds(i * 512, 512)]).then_inc(f_h, 1)

            def expand(i, e, wait):
                pe.wait_ge(f_g, i * (E * FC) + (e * FC + FC))
                if wait:
                    pe.wait_ge(f_x, i * (4 * E) + (4 * (e - 2) + 4))
                for t in range(4):
                    for j in range(FC):
                        last = mm(psum[4 + e % 2][:, t * P:(t + 1) * P], HT[:, e % 2, j, t * P:(t + 1) * P],
                                  w2_s[:, e, j, :], start=(j == 0), stop=(j == FC - 1))
                last.then_inc(f_y, 1)

            with pe.Fori(0, NT // 4) as i:
                hidden(i, 0, False)
                for e in range(E):
                    if e + 1 < E:
                        hidden(i, e + 1, e + 1 >= 2)
                    expand(i, e, e >= 2)
                pe.wait_ge(f_x, i * (4 * E) + 4 * E)

        @block.vector
        def _(dve):
            V = nc.vector
            chain = [0]

            def link(ins):
                chain[0] += 1
                ins.then_inc(dve_c, 1)
                dve.wait_ge(dve_c, chain[0])

            def moments_to_rstd(st_sem, rs_sem):
                me, mo = stats[:, :, 1], stats[:, :, 4]
                link(V.tensor_tensor(mv[:, :, 0], me, mo, ALU.add))
                link(V.tensor_scalar(mv[:, :, 0], mv[:, :, 0], 0.5, None, ALU.mult))
                link(V.tensor_tensor(mv[:, :, 1], me, mv[:, :, 0], ALU.subtract))
                link(V.tensor_tensor(mv[:, :, 1], mv[:, :, 1], mv[:, :, 1], ALU.mult))
                link(V.tensor_tensor(std[:, :], stats[:, :, 2], stats[:, :, 5], ALU.add))
                link(V.tensor_scalar(std[:, :], std[:, :], 1.0 / D, EPS, ALU.mult, ALU.add))
                V.tensor_tensor(std[:, :], std[:, :], mv[:, :, 1], ALU.add).then_inc(st_sem, 1)
                dve.wait_ge(rs_sem, 1)
                link(V.reciprocal(rstd[:, :], std[:, :]))

            def normalise(dst, src, tile):
                return V.tensor_scalar(dst, src,
                                       mv[:, bass.ds(tile, 1), 0], rstd[:, bass.ds(tile, 1)],
                                       ALU.subtract, ALU.mult)

            link(V.memset(thr[:, :], 0))
            for q in range(NLX):
                dve.wait_ge(ld_x, 16 * NLX) if q == 0 else None
            with dve.Fori(0, NT) as i:
                V.bn_stats(stats[:, bass.ds(i, 1), :].rearrange("p a s -> p (a s)"),
                           X[:, bass.ds(i, 1), :].rearrange("p a c -> p (a c)")).then_inc(dve_st1, 1)
            dve.wait_ge(dve_st1, NT)
            moments_to_rstd(n0_std, n0_rstd)
            dve.wait_ge(ld_w, NW)
            qv = sw_q[:, :].rearrange("p (k g a f) -> p g k a f", k=NG, g=4, a=2)
            kv = sw_k[:, :].rearrange("p (k a f) -> p k a f", k=NG, a=2)
            for g in range(4):
                for a in range(2):
                    for w, s in ((0, a), (1, 1 - a)):
                        dst = wqk[:, w, g * 32:(g + 1) * 32].rearrange("p (k a f) -> p k a f", k=NG, a=2)
                        V.tensor_copy(dst[:, :, a, :], qv[:, g, :, s, :])
                        dst = wqk[:, 2 + w, g * 32:(g + 1) * 32].rearrange("p (k a f) -> p k a f", k=NG, a=2)
                        last = V.tensor_copy(dst[:, :, a, :], kv[:, :, s, :])
            last.then_inc(wqk_ok, 1)
            def norm_queries(i):
                for h in range(2):
                    wait_reuse(dve, n0_tr, i * 2 + h)
                    for j in range(4):
                        t = i * 8 + (h * 4 + j)
                        normalise(xn[:, j, :], X[:, bass.ds(t, 1), :].rearrange("p a c -> p (a c)"), t)\
                            .then_inc(n0_xn, 1)
                    dve.wait_ge(n0_q, i * 2 + (h + 1))
                    V.tensor_scalar(QT[:, bass.ds((i * 2 + h) * 512, 512)], psum[2 + h][:, :],
                                    bias[:, 0:1], -SCALE, ALU.add, ALU.mult).then_inc(n0_qt, 1)

            peeled(dve, NT // 8, norm_queries)

            def mask_min(n, b, g, first):
                dve.wait_ge(pe_s, 4 * n + (g + 1))
                if g == 0:
                    dve.wait_ge(pool_m, n + 1)
                if not first:
                    dve.wait_ge(act_exp, 4 * n + (g - 3))
                V.memset(waited[:, g:g + 1], 0.0)
                V.tensor_tensor_reduce(SM[:, g, :], psum[2 + g % 2][:, 0:S2], MB[:, b % 2, :], 1.0, float(3e38),
                                       ALU.add, ALU.min, MN[:, g:g + 1]).then_inc(dve_min, 1)

            def evac_turned(m, b, g, first):
                dve.wait_ge(pe_t, 4 * m + (g + 1))
                if not (first and g < 2):
                    dve.wait_ge(pe_a, 4 * m + (g - 1))
                if g == 0:
                    V.tensor_copy(PTE[:, b % 2, :], psum[4][0:4, KC * P:KC * P + P])
                V.tensor_copy(PT[:, g % 2, :], psum[4 + g % 2][:, 0:KC * P]).then_inc(ev_t, 1)

            def evac_values(n, b):
                dve.wait_ge(pe_v, n + 1)
                V.tensor_copy(VT[:, b, :], psum[0][:, 0:KC * P])
                V.tensor_tensor(VE[:, b, :], psum[0][0:4, KC * P:KC * P + P], groupmask[:, :], ALU.mult)\
                    .then_inc(ev_v, 1)

            def evac_out(q, bank):
                dve.wait_ge(pe_a, 8 * q + 8)
                for s in range(2):
                    V.tensor_tensor(OM[:, s, :, :],
                                    psum[bank][:, s * P:(s + 1) * P].rearrange("p (h q) -> p h q", h=4),
                                    headmask[:, :].rearrange("p (a h) -> p h a", a=1).broadcast_to([P, 4, SQ]),
                                    ALU.mult).then_inc(dve_om, 1)
                dve.wait_ge(dve_om, 2 * q + 2)
                V.tensor_reduce(OT[:, bass.ds(q * 2 * SQ, 2 * SQ)].rearrange("p (s q) -> p s q", s=2),
                                OM[:, :, :, :].rearrange("p s h q -> p s q h"), AX_X, ALU.add)\
                    .then_inc(ev_o, 1)

            def batch(i, b, prev, more, first_tile):
                n = i * BT + b
                m, pb = n - 1, (b - 1) % BT
                mask_min(n, b, 0, first_tile and b == 0)
                if b % 2 == 1 and (b == 3 or not first_tile):
                    evac_out(i * 2 + (b - 3) // 2, 6 + (b // 2 + 1) % 2)
                if prev:
                    evac_turned(m, pb, 0, first_tile and b == 1)
                mask_min(n, b, 1, first_tile and b == 0)
                if prev:
                    evac_turned(m, pb, 1, first_tile and b == 1)
                mask_min(n, b, 2, first_tile and b == 0)
                if prev:
                    evac_turned(m, pb, 2, False)
                mask_min(n, b, 3, first_tile and b == 0)
                if prev:
                    evac_turned(m, pb, 3, False)
                if more:
                    evac_values(n + 1, (b + 1) % BT)

            evac_values(0, 0)
            for b in range(BT):
                batch(0, b, b > 0, True, True)
            with dve.Fori(1, NT - 1) as i:
                for b in range(BT):
                    batch(i, b, True, True, False)
            for b in range(BT):
                batch(NT - 1, b, True, b < BT - 1, False)
            for g in range(NG):
                evac_turned(NB - 1, BT - 1, g, False)
            evac_out(NB // 2 - 1, 7)

            dve.wait_ge(pe_rs, 1)
            for k in range(4):
                last = V.reciprocal(RIN[:, k, :, :].rearrange("p i g -> p (i g)"), psum[k][:, 0:NT * NG])
            last.then_inc(dve_rs, 1)
            dve.wait_ge(brow_pe, 1)
            V.tensor_tensor(brow[:, :], brow[:, :], psum[4][0:1, 0:P], ALU.add).then_inc(brow_ok, 1)
            dve.wait_ge(ev_o, NB // 2)
            with dve.Fori(0, NT // 2) as i:
                for h in range(2):
                    dve.wait_ge(pe_r, i * 2 + (h + 1))
                    V.tensor_tensor(OTN[:, h, :], OT[:, bass.ds((i * 2 + h) * P, P)], psum[h][:, 0:P],
                                    ALU.mult).then_inc(dve_otn, 1)
                for h in range(2):
                    dve.wait_ge(pe_x1, i * 2 + (h + 1))
                    xi = X[:, bass.ds(i * 2 + h, 1), :].rearrange("p a c -> p (a c)")
                    V.tensor_tensor(xi, xi, psum[2 + h][:, 0:P], ALU.add).then_inc(dve_x1, 1)
                for h in range(2):
                    dve.wait_ge(dve_x1, i * 2 + (h + 1))
                    V.bn_stats(stats[:, bass.ds(i * 2 + h, 1), :].rearrange("p a s -> p (a s)"),
                               X[:, bass.ds(i * 2 + h, 1), :].rearrange("p a c -> p (a c)")).then_inc(dve_st1, 1)
            dve.wait_ge(dve_st1, 2 * NT)
            moments_to_rstd(n1_std, n1_rstd)

            with dve.Fori(0, NT // 4) as i:
                for j in range(4):
                    t = i * 4 + j
                    normalise(xn[:, j, :], X[:, bass.ds(t, 1), :].rearrange("p a c -> p (a c)"), t)\
                        .then_inc(a_xn, 1)
                for j in range(4):
                    dve.wait_ge(a_pj, i * 4 + (j + 1))
                    for w in range(2):
                        V.tensor_tensor(
                            TQ[:, j, w::2, :].rearrange("p w (b s) -> p w b s", b=BT),
                            psum[4 + j][:, :].rearrange("p (w b s) -> p w b s", w=4, b=BT)[:, w::2],
                            rope[:, w, :].rearrange("p (c d s) -> p c d s", c=1, d=1)
                            .broadcast_to([P, 2, BT, SQ]), ALU.mult).then_inc(a_tq, 1)
                    V.tensor_tensor(VB[:, j, :, :, :],
                                    psum[j][:, P:2 * P].rearrange("p (b k d) -> p b k d", b=BT, k=NG),
                                    quadmask[:, :].rearrange("p (a k c) -> p a k c", a=1, c=1)
                                    .broadcast_to([P, BT, NG, HD]), ALU.mult).then_inc(a_vb, 1)
                    dve.wait_ge(a_tq, i * 8 + (2 * j + 2))
                    V.tensor_tensor(QKR[:, j, :, :], TQ[:, j, 0::2, :], TQ[:, j, 1::2, :], ALU.add)\
                        .then_inc(a_qk, 1)
                for j in range(4):
                    dve.wait_ge(a_s, i * 4 + (j + 1))
                    V.tensor_reduce(smx[:, j, :], psum[j][:, :].rearrange("p (n k) -> p n k", n=16), AX_X,
                                    ALU.max).then_inc(a_mx, 1)
                    dve.wait_ge(a_mx, i * 4 + (j + 1))
                    V.tensor_tensor(SX[:, j, :, :], psum[j][:, :].rearrange("p (n k) -> p n k", n=16),
                                    smx[:, j, :].rearrange("p (n a) -> p n a", a=1).broadcast_to([P, 16, SQ]),
                                    ALU.subtract).then_inc(a_sx, 1)
                for j in range(4):
                    dve.wait_ge(a_ex, i * 4 + (j + 1))
                    V.tensor_reduce(ssum[:, j, :], SX[:, j, :, :], AX_X, ALU.add).then_inc(a_sum, 1)
                    dve.wait_ge(a_sum, i * 4 + (j + 1))
                    V.reciprocal(sinv[:, j, :], ssum[:, j, :]).then_inc(a_inv, 1)
                for j in range(4):
                    dve.wait_ge(a_wo, i * 4 + (j + 1))
                    xi = X[:, bass.ds(i * 4 + j, 1), :].rearrange("p a c -> p (a c)")
                    V.tensor_tensor(xi, xi, psum[4 + j][:, 0:P], ALU.add).then_inc(a_x2, 1)
                for j in range(4):
                    dve.wait_ge(a_x2, i * 4 + (j + 1))
                    V.bn_stats(stats[:, bass.ds(i * 4 + j, 1), :].rearrange("p a s -> p (a s)"),
                               X[:, bass.ds(i * 4 + j, 1), :].rearrange("p a c -> p (a c)")).then_inc(a_st, 1)
            dve.wait_ge(a_st, NT)
            moments_to_rstd(n2_std, n2_rstd)

            def norm_router(i):
                for h in range(2):
                    wait_reuse(dve, r_tr, i * 2 + h)
                    for j in range(4):
                        t = i * 8 + (h * 4 + j)
                        normalise(xn[:, j, :], X[:, bass.ds(t, 1), :].rearrange("p a c -> p (a c)"), t)\
                            .then_inc(r_xn, 1)
                    dve.wait_ge(r_lg, i * 2 + (h + 1))
                    V.tensor_copy(PRB[:, bass.ds(i * 8 + h * 4, 4), :].rearrange("p i e -> p (i e)"),
                                  psum[2 + h][:, 0:4 * E]).then_inc(r_cp, 1)

            peeled(dve, NT // 8, norm_router)
            dve.wait_ge(r_cp, NT // 4)

            def over_experts(v):
                return v.rearrange("p (i a) -> p i a", a=1).broadcast_to([P, NT, E])

            link(V.tensor_reduce(rmx[:, :], PRB[:, :, :], AX_X, ALU.max))
            V.tensor_tensor(PRB[:, :, :], PRB[:, :, :], over_experts(rmx[:, :]), ALU.subtract).then_inc(t_act, 1)
            dve.wait_ge(t_exp, 1)
            link(V.tensor_reduce(rmx[:, :], PRB[:, :, :], AX_X, ALU.add))
            link(V.reciprocal(any_[:, :], rmx[:, :]))
            V.tensor_tensor(PRB[:, :, :], PRB[:, :, :], over_experts(any_[:, :]), ALU.mult).then_inc(t_dve, 1)
            dve.wait_ge(t_pe, 1)
            link(V.tensor_copy(PRT[:, :, :].rearrange("p a t -> p (a t)"), psum[0][:, 0:HALVES * P]))
            prt = PRT[:, :, :].rearrange("p a t -> p (a t)")
            cmpf = cmp_[:, :, :].rearrange("p a t -> p (a t)")

            for k, bit in enumerate(bits):
                link(V.tensor_scalar(thr_try[:, :], thr[:, :], 1 << bit, None, ALU.bitwise_or))
                V.tensor_scalar(cmpf, prt, thr_try[:, :].bitcast(F32), 0.0, ALU.is_ge, ALU.add,
                                accum_out=cnt[:, :]).then_inc(t_dve, 1)
                dve.wait_ge(t_pe, 2 + k)
                link(V.tensor_scalar(bit_ok[:, :], psum[1][:, 0:1], CAP - 0.5, float(1 << bit),
                                     ALU.is_ge, ALU.mult))
                link(V.tensor_tensor(thr[:, :], thr[:, :], bit_ok[:, :], ALU.bitwise_or))
            nb = len(bits)
            thf = thr[:, :].bitcast(F32)
            V.tensor_scalar(GT[:, :, :].rearrange("p a t -> p (a t)"), prt, thf, 0.0, ALU.is_gt, ALU.add,
                            accum_out=cnt[:, :]).then_inc(t_dve, 1)
            dve.wait_ge(t_pe, 2 + nb)
            link(V.tensor_scalar(need[:, 0:1], psum[2][:, 0:1], -1.0, float(CAP), ALU.mult, ALU.add))
            for a in range(HALVES):
                link(V.tensor_scalar(EQ[:, a, :], PRT[:, a, :], thf, 0.0, ALU.is_equal, ALU.add,
                                     accum_out=tot[:, a:a + 1]))
            V.memset(cmpf, 0.0).then_inc(t_dve, 1)
            dve.wait_ge(t_pe, 3 + nb)
            link(V.tensor_copy(need[:, 1:2], need[:, 0:1]))
            link(V.tensor_tensor(need[:, :], need[:, :], psum[3][:, 0:HALVES], ALU.subtract))
            for a in range(HALVES):
                link(V.tensor_tensor_scan(PFX[:, a, :], EQ[:, a, :], zero_row[:, :], 0.0, ALU.add, ALU.add))
                link(V.tensor_scalar(PFX[:, a, :], PFX[:, a, :], need[:, a:a + 1], None, ALU.is_le))
            link(V.tensor_tensor(PFX[:, :, :], PFX[:, :, :], EQ[:, :, :], ALU.mult))
            V.tensor_tensor(GT[:, :, :], GT[:, :, :], PFX[:, :, :], ALU.add).then_inc(t_dve, 1)
            dve.wait_ge(t_pe, 4 + nb)
            link(V.tensor_copy(SEL[:, :, :].rearrange("p i e -> p (i e)"), psum[0][:, 0:HALVES * P]))
            link(V.tensor_tensor(KEY[:, :, :], PRB[:, :, :], SEL[:, :, :], ALU.mult))
            link(V.tensor_scalar(RT[:, :, :], SEL[:, :, :], -1.0, None, ALU.add))
            link(V.tensor_tensor(KEY[:, :, :], KEY[:, :, :], RT[:, :, :], ALU.add))
            link(V.tensor_reduce(any_[:, :], KEY[:, :, :], AX_X, ALU.max))
            link(V.tensor_scalar(rmx[:, :], any_[:, :], 0.0, None, ALU.is_lt))
            link(V.tensor_scalar(any_[:, :], any_[:, :], 0.0, None, ALU.is_ge))
            link(V.tensor_tensor(KEY[:, :, :], KEY[:, :, :], over_experts(any_[:, :]), ALU.mult))
            link(V.tensor_tensor(RT[:, :, :], PRB[:, :, :], over_experts(rmx[:, :]), ALU.mult))
            link(V.tensor_tensor(KEY[:, :, :], KEY[:, :, :], RT[:, :, :], ALU.add))
            link(V.tensor_reduce(rmx[:, :], KEY[:, :, :], AX_X, ALU.max))
            link(V.tensor_tensor(KEY[:, :, :], KEY[:, :, :], over_experts(rmx[:, :]), ALU.is_equal))
            by_rank = rank[:, :].rearrange("p (a e) -> p a e", a=1).broadcast_to([P, NT, E])
            link(V.tensor_tensor(KEY[:, :, :], KEY[:, :, :], by_rank, ALU.mult))
            link(V.tensor_reduce(rmx[:, :], KEY[:, :, :], AX_X, ALU.max))
            link(V.tensor_tensor(KEY[:, :, :], by_rank, over_experts(rmx[:, :]), ALU.is_equal))
            V.tensor_tensor(GATE[:, :, :], KEY[:, :, :], PRB[:, :, :], ALU.mult).then_inc(t_done, 1)
            dve.wait_ge(t_done, 1)

            with dve.Fori(0, NT // 4) as i:
                for e in range(E):
                    dve.wait_ge(f_y, i * E + (e + 1))
                    if e:
                        dve.wait_ge(f_x, i * (4 * E) + 4 * e)
                    for t in range(4):
                        xi = X[:, bass.ds(i * 4 + t, 1), :].rearrange("p a c -> p (a c)")
                        V.scalar_tensor_tensor(xi, psum[4 + e % 2][:, t * P:(t + 1) * P],
                                               GATE[:, bass.ds(i * 4 + t, 1), e], xi, ALU.mult, ALU.add)\
                            .then_inc(f_x, 1)


_INS = ["x", "ctx_1024", "mask_BxSxS2_ik1", "L0_xattn_Wq", "L0_xattn_bq", "L0_xattn_Wk", "L0_xattn_bk",
        "L0_xattn_Wv", "L0_xattn_bv", "L0_xattn_Wo", "L0_xattn_bo", "L0_attn_w_q", "L0_attn_w_k",
        "L0_attn_w_v", "L0_attn_w_o", "L0_ffn_Wg", "L0_ffn_W1", "L0_ffn_W2"]


def kernel(**inputs):
    import concourse.bacc as bacc
    from concourse.bass_utils import run_bass_kernel_spmd

    nc = bacc.Bacc("TRN2", target_bir_lowering=False, num_devices=1)
    arrays, args = {}, []
    for name in _INS:
        a = np.ascontiguousarray(inputs[name])
        arrays["in_" + name] = a
        args.append(nc.dram_tensor("in_" + name, a.shape, mybir.dt.from_np(a.dtype), kind="ExternalInput").ap())
    B, S, D = inputs["x"].shape
    table = shape_constants(B, S)
    for name in _CONSTS:
        a = np.ascontiguousarray(table[name])
        arrays["const_" + name] = a
        args.append(nc.dram_tensor("const_" + name, a.shape, F32, kind="ExternalInput").ap())
    args.append(nc.dram_tensor("out", (B, S, D), F32, kind="ExternalOutput").ap())
    perceiver_block(nc, *args)
    r = run_bass_kernel_spmd(nc, [arrays], core_ids=[0])
    return r.results[0]["out"]
```

```python
from contextlib import ExitStack

import numpy as np

import concourse.bass as bass
from concourse import mybir

F32 = mybir.dt.float32
I32 = mybir.dt.int32
ALU = mybir.AluOpType
ACT = mybir.ActivationFunctionType
AX_X = mybir.AxisListType.X

P = 128
HD = 8
NG = 4
SQ = 32
BT = P // SQ
BIG = float(2.0 ** 100)
EPS = 1e-5


def shape_constants(B, S):
    c = np.arange(P)
    one = np.float32
    out = {}
    out["ident"] = np.eye(P, dtype=one)
    out["headmask"] = (((c % 32) // HD)[:, None] == np.arange(4)[None, :]).astype(one)
    out["ownhead"] = ((c // HD)[:, None] == np.arange(16)[None, :]).astype(one)
    out["groupmask"] = (np.arange(4)[:, None] == (c // 32)[None, :]).astype(one)
    out["quadmask"] = ((c // 32)[:, None] == np.arange(4)[None, :]).astype(one)
    f = (c % HD) % 4
    inv = (1.0 / np.float32(10000.0) ** (np.arange(4, dtype=one) * 2.0 / HD)).astype(one)
    ang = (np.arange(S, dtype=one)[None, :] * inv[f][:, None]).astype(one)
    sign = np.where(c % HD < 4, -1.0, 1.0).astype(one)[:, None]
    out["rope"] = np.concatenate([np.cos(ang), np.sin(ang) * sign], axis=1).astype(one)
    e, t = c % 8, c // 8
    same = e[:, None] == e[None, :]
    out["same_expert"] = same.astype(one)
    out["earlier_tile"] = (same & (t[:, None] < t[None, :])).astype(one)
    out["rank"] = np.broadcast_to(8.0 - np.arange(8), (P, 8)).astype(one).copy()
    return out


_CONSTS = ["ident", "headmask", "ownhead", "groupmask", "quadmask", "rope", "same_expert", "earlier_tile", "rank"]


def perceiver_block(nc, x, ctx_in, mask, Wq, bq, Wk, bk, Wv, bv, Wo, bo,
                    w_q, w_k, w_v, w_o, Wg, W1, W2,
                    c_ident, c_head, c_own, c_group, c_quad, c_rope, c_same, c_earlier, c_rank, out):
    NB, S, D = x.shape
    S2 = ctx_in.shape[1]
    T = NB * S
    NT = T // P
    KC = (S2 - 1) // P
    E, F = Wg.shape[1], W1.shape[2]
    FC = F // P
    CAP = max(1, T // E)
    assert (D, S, NB % BT, S2 - KC * P, E) == (P, SQ, 0, 1, 8)
    SCALE = 1.0 / float(np.sqrt(np.float32(HD)))
    HALVES = NT // 16

    with ExitStack() as ctx:
        def sb(name, shape, dt=F32):
            return ctx.enter_context(nc.sbuf_tensor(name, shape, dt))

        def sem(name):
            return ctx.enter_context(nc.semaphore(name))

        psum = [ctx.enter_context(nc.psum_tensor(f"bank{i}", [P, 512], F32)) for i in range(8)]

        ident = sb("ident", [P, P])
        headmask = sb("headmask", [P, 4])
        ownhead = sb("ownhead", [P, 16])
        groupmask = sb("groupmask", [4, P])
        quadmask = sb("quadmask", [P, 4])
        rope = sb("rope", [P, 2, S])
        same = sb("same", [P, P])
        earlier = sb("earlier", [P, P])
        rank = sb("rank", [P, 8])
        wq_s = sb("wq_s", [P, P])
        wk_s = sb("wk_s", [P, P])
        wv_s = sb("wv_s", [P, P])
        wo_s = sb("wo_s", [P, P])
        bias = sb("bias", [P, 3])
        bo_s = sb("bo_s", [1, P])
        brow = sb("brow", [1, P])
        BROW = sb("BROW", [P, P])
        qbias = sb("qbias", [P, 1])
        ones1 = sb("ones1", [1, P])
        sw_q = sb("sw_q", [P, P])
        sw_k = sb("sw_k", [P, NG * HD])
        sw_v = sb("sw_v", [P, NG * HD])
        sw_o = sb("sw_o", [P, P])
        wqk = sb("wqk", [P, 4, P])
        wg_s = sb("wg_s", [P, E])
        w1_s = sb("w1_s", [P, E, F])
        w2_s = sb("w2_s", [P, E, FC, P])

        X = sb("X", [P, NT, P])
        QT = sb("QT", [P, T])
        OT = sb("OT", [P, T])
        XTT = QT
        stats = sb("stats", [P, NT, 6])
        mv = sb("mv", [P, NT, 2])
        std = sb("std", [P, NT])
        rstd = sb("rstd", [P, NT])
        shift = sb("shift", [P, NT])
        RSUM = sb("RSUM", [P, NT, BT, NG])
        RIN = sb("RIN", [P, 4, NT, NG])

        xn = sb("xn", [P, 2, 4, P])
        xg = sb("xg", [P, 2, 512])

        CX = sb("CX", [P, BT, KC, P])
        CXE = sb("CXE", [1, BT, P])
        MK = sb("MK", [P, BT, S2], I32)
        MB = sb("MB", [P, BT, S2])
        CT = sb("CT", [P, 2, S2])
        KT = sb("KT", [P, 2, S2])
        VT = sb("VT", [P, BT, KC * P])
        VR = sb("VR", [4, BT, P])
        VE = sb("VE", [4, BT, P])
        QB = sb("QB", [P, BT, NG * 4, SQ])
        SM = sb("SM", [P, NG, S2])
        MN = sb("MN", [P, NG])
        PR = sb("PR", [P, 2, NG, S2])
        PT = sb("PT", [P, 2, KC * P])
        PTE = sb("PTE", [4, 2, P])
        OC = sb("OC", [P, 2, 2 * P])

        xt = sb("xt", [P, 4, P])
        TQ = sb("TQ", [P, 4, 4, P])
        QKR = sb("QKR", [P, 4, 2, P])
        QD = sb("QD", [P, 4, BT, 4, SQ])
        KB = sb("KB", [P, 4, BT, NG, SQ])
        VB = sb("VB", [P, 4, BT, NG, HD])
        SX = sb("SX", [P, 4, 16, SQ])
        smx = sb("smx", [P, 4, 16])
        ssum = sb("ssum", [P, 4, 16])
        sinv = sb("sinv", [P, 4, 16])
        SP = sb("SP", [P, 4, BT, P])
        SO = sb("SO", [P, 4, P])
        RIE = xt
        OTN = SO

        PRB = sb("PRB", [P, NT, E])
        rmx = sb("rmx", [P, NT])
        PRT = sb("PRT", [P, HALVES, P])
        assert HALVES == 2
        cmp_, GT, EQ, PFX = (QKR[:, k, :, :] for k in range(4))
        cnt = sb("cnt", [P, 1])
        thr = sb("thr", [P, 1], I32)
        thr_try = sb("thr_try", [P, 1], I32)
        bit_ok = sb("bit_ok", [P, 1], I32)
        tot = sb("tot", [P, 2])
        need = sb("need", [P, 2])
        SEL = sb("SEL", [P, NT, E])
        KEY = sb("KEY", [P, NT, E])
        RT = sb("RT", [P, NT, E])
        any_ = sb("any_", [P, NT])
        GATE = sb("GATE", [P, NT, E])
        HT = sb("HT", [P, 2, FC, 512])
        zero_row = sb("zero_row", [P, P])
        warm = sb("warm", [1, 1])
        waited = sb("waited", [1, NG])

        NLX = 4
        ld_x = [sem(f"ld_x{j}") for j in range(NLX)]
        ld_w = sem("ld_w")
        ld_ffn = sem("ld_ffn")
        dve_c = sem("dve_c")
        n0_std = sem("n0_std")
        n0_rstd = sem("n0_rstd")
        n0_xn = sem("n0_xn")
        n0_tr = sem("n0_tr")
        n0_xt = sem("n0_xt")
        n0_q = sem("n0_q")
        n0_qt = sem("n0_qt")
        warm_ok = sem("warm_ok")
        x_biased = sem("x_biased")
        brow_all = sem("brow_all")
        brow_sp = sem("brow_sp")
        n0_bias = sem("n0_bias")

        ld_ctx = [sem(f"ld_ctx{b}") for b in range(BT)]
        ld_mask = [sem(f"ld_mask{b}") for b in range(BT)]
        pe_l = sem("pe_l")
        pe_k = sem("pe_k")
        pe_v = sem("pe_v")
        pe_s = sem("pe_s")
        pe_t = sem("pe_t")
        pe_a = sem("pe_a")
        ev_l = sem("ev_l")
        ev_k = sem("ev_k")
        ev_v = sem("ev_v")
        ev_t = sem("ev_t")
        ev_o = sem("ev_o")
        ev_w = sem("ev_w")
        ev_e = sem("ev_e")
        pe_e = sem("pe_e")
        pe_o = sem("pe_o")
        pool_c = sem("pool_c")
        pool_o = sem("pool_o")
        dve_min = sem("dve_min")
        act_exp = sem("act_exp")
        pool_q = sem("pool_q")
        pool_m = sem("pool_m")

        pe_rs = sem("pe_rs")
        dve_rs = sem("dve_rs")
        pool_r = sem("pool_r")
        pe_r = sem("pe_r")
        dve_otn = sem("dve_otn")
        pe_x1 = sem("pe_x1")
        dve_x1 = sem("dve_x1")
        dve_st1 = sem("dve_st1")
        brow_pe = sem("brow_pe")
        brow_ok = sem("brow_ok")
        n1_std = sem("n1_std")
        n1_rstd = sem("n1_rstd")
        n1_shift = sem("n1_shift")

        a_xn = sem("a_xn")
        a_tr = sem("a_tr")
        a_p = sem("a_p")
        a_v = sem("a_v")
        zero_ok = sem("zero_ok")
        ones_ok = sem("ones_ok")
        a_xt = sem("a_xt")
        a_tq = sem("a_tq")
        a_qk = sem("a_qk")
        a_vb = sem("a_vb")
        a_kb = sem("a_kb")
        a_qd = sem("a_qd")
        a_s = sem("a_s")
        a_mx = sem("a_mx")
        a_sx = sem("a_sx")
        a_ex = sem("a_ex")
        a_sum = sem("a_sum")
        a_inv = sem("a_inv")
        a_pn = sem("a_pn")
        a_pt = sem("a_pt")
        a_sp = sem("a_sp")
        a_o = sem("a_o")
        a_so = sem("a_so")
        a_wo = sem("a_wo")
        a_x2 = sem("a_x2")
        a_st = sem("a_st")
        wqk_ok = sem("wqk_ok")
        n2_std = sem("n2_std")
        n2_rstd = sem("n2_rstd")

        r_xn = sem("r_xn")
        r_tr = sem("r_tr")
        r_xt = sem("r_xt")
        r_xtt = sem("r_xtt")
        r_lg = sem("r_lg")
        r_cp = sem("r_cp")
        t_act = sem("t_act")
        t_exp = sem("t_exp")
        t_pe = sem("t_pe")
        t_dve = sem("t_dve")
        t_done = sem("t_done")
        f_h = sem("f_h")
        f_g = sem("f_g")
        f_y = sem("f_y")
        f_x = sem("f_x")
        st_out = sem("st_out")

        block = ctx.enter_context(nc.Block())

        x_tiles = x.rearrange("(i b) s d -> (b s) i d", b=BT)
        out_tiles = out.rearrange("(i b) s d -> (b s) i d", b=BT)
        bits = list(range(29, -1, -1))

        def wait_reuse(eng, s, v):
            if not (isinstance(v, int) and v <= 0):
                eng.wait_ge(s, v)

        def pipeline(eng, stages, n, width, lags):
            def step(t, j):
                for lag, body in stages:
                    if not isinstance(t, int) or 0 <= t - lag < n:
                        body(t - lag, (j - lag) % width)

            fill = width * ((lags + width - 1) // width + 1)
            for t in range(fill):
                step(t, t % width)
            if n // width - 1 > fill // width:
                with eng.Fori(fill // width, n // width - 1) as i:
                    for j in range(width):
                        step(i * width + j, j)
            for t in range(max(fill, n - width), n + lags):
                step(t, t % width)

        def mm(o, l, r, start=True, stop=True):
            return nc.tensor.matmul(o, l, r, start=start, stop=stop, skip_group_check=True)

        def tr(o, i, n=P):
            return nc.tensor.transpose(o, i, ident[0:n, 0:n])

        small = [(wq_s, Wq), (wk_s, Wk), (wv_s, Wv), (wo_s, Wo), (ident, c_ident), (headmask, c_head), (ownhead, c_own),
                 (groupmask, c_group), (quadmask, c_quad), (same, c_same), (earlier, c_earlier),
                 (rank, c_rank), (sw_q, w_q), (sw_k, w_k), (sw_v, w_v), (wg_s, Wg)]
        NW = 16 * (len(small) + 6 + 3 + 1)

        @block.sync
        def _(sp):
            for j in range(NLX):
                n = NT // NLX
                sp.dma_start(X[:, j * n:(j + 1) * n, :], x_tiles[:, j * n:(j + 1) * n, :]).then_inc(ld_x[j], 16)

            def load_batch(i, b, first):
                if not first:
                    sp.wait_ge(pe_l, i * BT + (b - BT + 1))
                sp.dma_start(CX[:, b, :, :], ctx_in[bass.ds(i * BT + b, 1), 0:KC * P, :]
                             .rearrange("a (j p) c -> p (a j) c", p=P)).then_inc(ld_ctx[b], 16)
                sp.dma_start(CXE[0:1, b, :], ctx_in[bass.ds(i * BT + b, 1), KC * P, :]).then_inc(ld_ctx[b], 16)
                if not first:
                    sp.wait_ge(pool_m, i * BT + (b - BT + 1))
                for r in range(4):
                    sp.dma_start(MK[r * SQ:(r + 1) * SQ, b, :],
                                 mask[bass.ds(i * BT + b, 1), :, :].rearrange("a q k -> (a q) k"))\
                        .then_inc(ld_mask[b], 16)

            for b in range(BT):
                load_batch(0, b, True)
            with sp.Fori(1, NT) as i:
                for b in range(BT):
                    load_batch(i, b, False)
            sp.dma_start(w1_s[:, :, :], W1.rearrange("e c f -> c e f")).then_inc(ld_ffn, 16)
            sp.dma_start(w2_s[:, :, :, :], W2.rearrange("e (j f) c -> f e j c", f=P)).then_inc(ld_ffn, 16)
            with sp.Fori(0, NT // 4) as g:
                sp.wait_ge(f_x, (g + 1) * (4 * E))
                sp.dma_start(out_tiles[:, bass.ds(g * 4, 4), :], X[:, bass.ds(g * 4, 4), :]).then_inc(st_out, 16)
            sp.wait_ge(st_out, 16 * (NT // 4))

        @block.scalar
        def _(act):
            for dst, src in small:
                act.dma_start(dst[:, :], src).then_inc(ld_w, 16)
            for j, bvec in enumerate((bq, bk, bv)):
                act.dma_start(bias[:, j:j + 1], bvec.rearrange("(c a) -> c a", a=1)).then_inc(ld_w, 16)
            act.dma_start(bo_s[:, :], bo.rearrange("(a c) -> a c", a=1)).then_inc(ld_w, 16)
            act.dma_start(rope[:, :, :], c_rope.rearrange("p (a s) -> p a s", a=2)).then_inc(ld_w, 16)
            for g in range(NG):
                act.dma_start(sw_o[g * 32:(g + 1) * 32, :],
                              w_o.rearrange("(k g d) c -> g k d c", k=NG, g=4)[g]).then_inc(ld_w, 16)
            act.dma_start(brow[:, :], bo.rearrange("(a c) -> a c", a=1)).then_inc(ld_w, 16)

            act.wait_ge(warm_ok, 1)
            act.wait_ge(n0_std, 1)
            nc.scalar.activation(std[:, :], std[:, :], ACT.Sqrt).then_inc(n0_rstd, 1)

            def evac_x(u, h):
                act.wait_ge(n0_tr, u + 1)
                wait_reuse(act, n0_q, u - 1)
                nc.scalar.activation(xg[:, h, :], psum[h][:, :], ACT.Copy).then_inc(n0_xt, 1)

            def evac_q(u, h):
                act.wait_ge(n0_q, u + 1)
                nc.scalar.activation(QT[:, bass.ds(u * 512, 512)], psum[2 + h][:, :], ACT.Identity,
                                     bias=qbias[:, :], scale=-SCALE).then_inc(n0_qt, 1)

            act.wait_ge(n0_bias, 1)
            pipeline(act, [(0, evac_x), (1, evac_q)], NT // 4, 2, 2)

            def evac_ctx(n, b):
                act.wait_ge(pe_l, n + 1)
                nc.scalar.activation(CT[:, b % 2, :], psum[0][:, 0:S2], ACT.Copy).then_inc(ev_l, 1)

            def evac_k(n, b):
                act.wait_ge(pe_k, n + 1)
                nc.scalar.activation(KT[:, b % 2, :], psum[1][:, 0:S2], ACT.Identity,
                                     bias=bias[:, 1:2]).then_inc(ev_k, 1)

            def exp_group(n, i, b, g):
                act.wait_ge(dve_min, 4 * n + (g + 1))
                nc.scalar.activation(PR[:, b % 2, g, :], SM[:, g, :], ACT.Exp, bias=MN[:, g:g + 1], scale=-1.0,
                                     accum_out=RSUM[:, bass.ds(i, 1), b, g:g + 1].rearrange("p a g -> p (a g)"))\
                    .then_inc(act_exp, 1)

            def evac_last_key(m, b):
                act.wait_ge(pe_e, m + 1)
                nc.scalar.activation(PTE[:, b % 2, :], psum[1][0:4, 3 * P:4 * P], ACT.Copy).then_inc(ev_e, 1)

            def evac_values(n, b):
                act.wait_ge(pe_v, n + 1)
                nc.scalar.activation(VT[:, b, :], psum[0][:, 0:KC * P], ACT.Copy)
                nc.scalar.activation(VR[:, b, :], psum[0][0:4, KC * P:KC * P + P], ACT.Copy).then_inc(ev_w, 1)

            def evac_out(q, bank, first):
                act.wait_ge(pe_o, 2 * q + 2)
                if not first:
                    act.wait_ge(pool_o, q - 1)
                nc.scalar.activation(OC[:, bank % 2, :], psum[bank][:, 0:2 * P], ACT.Copy).then_inc(ev_o, 1)

            def batch(i, b, more, first_tile, second_tile=False):
                n = i * BT + b
                nb = (b + 1) % BT
                exp_group(n, i, b, 0)
                if more:
                    evac_ctx(n + 1, nb)
                exp_group(n, i, b, 1)
                if more:
                    evac_k(n + 1, nb)
                if b % 2 == 1 and (b == 3 or not first_tile):
                    evac_out(i * 2 + (b - 3) // 2, 6 + (b == 1), first_tile or (second_tile and b == 1))
                exp_group(n, i, b, 2)
                if more:
                    evac_values(n + 1, nb)
                exp_group(n, i, b, 3)
                if not first_tile or b >= 1:
                    evac_last_key(n - 1, (b - 1) % BT)

            nc.scalar.activation(warm[:, :], warm[:, :], ACT.Exp)
            evac_ctx(0, 0)
            evac_k(0, 0)
            evac_values(0, 0)
            for b in range(BT):
                batch(0, b, True, True)
            for b in range(BT):
                batch(1, b, True, False, True)
            with act.Fori(2, NT - 1) as i:
                for b in range(BT):
                    batch(i, b, True, False)
            for b in range(BT):
                batch(NT - 1, b, b < BT - 1, False)
            evac_last_key(NB - 1, BT - 1)
            evac_out(NB // 2 - 1, 7, False)

            act.wait_ge(n1_std, 1)
            nc.scalar.activation(std[:, :], std[:, :], ACT.Sqrt).then_inc(n1_rstd, 1)

            nc.scalar.activation(warm[:, :], warm[:, :], ACT.Exp)

            def centre(t, j):
                wait_reuse(act, a_tr, t - 3)
                nc.scalar.activation(xn[:, 0, j, :], X[:, bass.ds(t, 1), :].rearrange("p a c -> p (a c)"), ACT.Identity,
                                     bias=shift[:, bass.ds(t, 1)], scale=rstd[:, bass.ds(t, 1)]).then_inc(a_xn, 1)

            def evac_xt(t, j):
                act.wait_ge(a_tr, t + 1)
                wait_reuse(act, a_v, t - 3)
                nc.scalar.activation(xt[:, j, :], psum[0][:, 0:P], ACT.Copy).then_inc(a_xt, 1)

            def exp_scores(t, j):
                act.wait_ge(a_sx, t + 1)
                nc.scalar.activation(SX[:, j, :, :], SX[:, j, :, :], ACT.Exp, scale=SCALE).then_inc(a_ex, 1)

            def evac_probs(t, j):
                act.wait_ge(a_pt, t + 1)
                wait_reuse(act, a_o, t - 3)
                nc.scalar.activation(SP[:, j, :, :].rearrange("p b k -> p (b k)"), psum[6][:, :],
                                     ACT.Copy).then_inc(a_sp, 1)

            def evac_o(t, j):
                act.wait_ge(a_o, t + 1)
                wait_reuse(act, a_wo, t - 3)
                nc.scalar.activation(SO[:, j, :], psum[7][:, 0:P], ACT.Copy).then_inc(a_so, 1)

            def own_values(t, j):
                act.wait_ge(a_v, t + 1)
                wait_reuse(act, a_o, t - 3)
                for g in range(NG):
                    rows = slice(g * 32, g * 32 + 32)
                    last = nc.scalar.activation(VB[rows, j, :, g, :],
                                                psum[1][rows, 0:P].rearrange("p (b k d) -> p b k d", b=BT, k=NG)
                                                [:, :, g, :], ACT.Copy)
                last.then_inc(a_vb, 1)

            def own_keys(t, j):
                act.wait_ge(a_qk, t + 1)
                wait_reuse(act, a_s, t - 3)
                for g in range(NG):
                    rows = slice(g * 32, g * 32 + 32)
                    last = nc.scalar.activation(KB[rows, j, :, g, :],
                                                QKR[rows, j, 1, :].rearrange("p (b k) -> p b k", b=BT), ACT.Copy)
                last.then_inc(a_kb, 1)

            act.wait_ge(zero_ok, 1)
            act.wait_ge(n1_shift, 1)
            centre(0, 0)
            pipeline(act, [(5, evac_probs), (0, evac_xt), (2, own_keys), (3, exp_scores), (5, evac_o), (1, own_values),
                           (-1, centre)], NT, 4, 6)

            act.wait_ge(n2_std, 1)
            nc.scalar.activation(std[:, :], std[:, :], ACT.Sqrt).then_inc(n2_rstd, 1)

            def evac_router(u, h):
                act.wait_ge(r_tr, u + 1)
                wait_reuse(act, r_lg, u - 1)
                nc.scalar.activation(xg[:, h, :], psum[h][:, :], ACT.Copy).then_inc(r_xt, 1)
                nc.scalar.activation(XTT[:, bass.ds(u * 512, 512)], psum[h][:, :], ACT.Copy).then_inc(r_xtt, 1)

            pipeline(act, [(0, evac_router)], NT // 4, 2, 2)
            act.wait_ge(t_act, 1)
            nc.scalar.activation(PRB[:, :, :], PRB[:, :, :], ACT.Exp).then_inc(t_exp, 1)

            nc.scalar.activation(warm[:, :], warm[:, :], ACT.Gelu)
            with act.Fori(0, NT // 4) as i:
                for e in range(E):
                    for j in range(FC):
                        act.wait_ge(f_h, i * (E * FC) + (e * FC + j + 1))
                        if j == 0 and e >= 2:
                            act.wait_ge(f_y, i * E + (e - 1))
                        nc.scalar.activation(HT[:, e % 2, j, :], psum[2 * (e % 2) + j][:, :], ACT.Gelu)\
                            .then_inc(f_g, 1)

        @block.gpsimd
        def _(pool):
            nc.gpsimd.memset(warm[:, :], 0.0).then_inc(warm_ok, 1)
            nc.gpsimd.memset(ones1[:, :], 1.0).then_inc(ones_ok, 1)
            nc.gpsimd.memset(zero_row[:, :], 0.0)
            nc.gpsimd.memset(KB[:, :, :, :, :], 0.0)
            nc.gpsimd.memset(VB[:, :, :, :, :], 0.0).then_inc(zero_ok, 1)

            pool.wait_ge(ld_w, NW)
            pool.wait_ge(n0_qt, NT // 4)

            def prepare(n, b, first):
                if not first:
                    pool.wait_ge(pe_s, 4 * n - 12)
                    pool.wait_ge(dve_min, 4 * n - 12)
                pool.wait_ge(ld_mask[b], 64 * (n // BT) + 64 if isinstance(n, int) else 16 * (n - b) + 64)
                nc.gpsimd.tensor_tensor(
                    QB[:, b, :, :],
                    QT[:, bass.ds(n * SQ, SQ)].rearrange("p (a q) -> p a q", a=1).broadcast_to([P, 16, SQ]),
                    ownhead[:, :].rearrange("p (a h) -> p h a", a=1).broadcast_to([P, 16, SQ]),
                    ALU.mult).then_inc(pool_q, 1)
                nc.gpsimd.tensor_scalar(MB[:, b, :], MK[:, b, :], 0.0, BIG, ALU.is_equal, ALU.mult)\
                    .then_inc(pool_m, 1)

            def last_key_values(m, b):
                pool.wait_ge(ev_w, m + 1)
                nc.gpsimd.tensor_tensor(VE[:, b, :], VR[:, b, :], groupmask[:, :], ALU.mult).then_inc(ev_v, 1)

            def keep_own(q, k):
                pool.wait_ge(ev_o, q + 1)
                own = OC[:, k, :].rearrange("p (s h q) -> p s h q", s=2, h=4)
                for s in range(2):
                    nc.gpsimd.tensor_tensor(
                        own[:, s], own[:, s],
                        headmask[:, :].rearrange("p (a h) -> p h a", a=1).broadcast_to([P, 4, SQ]),
                        ALU.mult).then_inc(pool_c, 1)
                pool.wait_ge(pool_c, 4 * q + 2)
                nc.gpsimd.tensor_tensor(own[:, :, 0:2], own[:, :, 0:2], own[:, :, 2:4], ALU.add).then_inc(pool_c, 2)
                pool.wait_ge(pool_c, 4 * q + 4)
                nc.gpsimd.tensor_tensor(OT[:, bass.ds(q * 2 * SQ, 2 * SQ)].rearrange("p (s q) -> p s q", s=2),
                                        own[:, :, 0], own[:, :, 1], ALU.add).then_inc(pool_o, 1)

            def tile(i):
                for b in range(BT):
                    n = i * BT + b
                    prepare(n, b, isinstance(i, int) and i == 0)
                    if not (isinstance(i, int) and n < 2):
                        last_key_values(n - 2, (b - 2) % BT)
                    if b % 2 == 1 and not (isinstance(i, int) and n < 5):
                        keep_own(i * 2 + (b - 5) // 2, int(b == 3))

            tile(0)
            pool.wait_ge(brow_sp, 1)
            nc.gpsimd.tensor_tensor(X[:, :, :], X[:, :, :],
                                    BROW[:, :].rearrange("p (a c) -> p a c", a=1).broadcast_to([P, NT, P]),
                                    ALU.add).then_inc(x_biased, 1)
            tile(1)
            with pool.Fori(2, NT) as i:
                tile(i)
            last_key_values(NB - 2, BT - 2)
            last_key_values(NB - 1, BT - 1)
            keep_own(NB // 2 - 2, 0)
            keep_own(NB // 2 - 1, 1)

            pool.wait_ge(dve_rs, 1)
            def spread(t, j):
                wait_reuse(pool, pe_r, t - 3)
                nc.gpsimd.tensor_copy(
                    RIE[:, j, :].rearrange("p (g k d) -> p g k d", g=NG, k=4),
                    RIN[:, :, bass.ds(t, 1), :].rearrange("p k a g -> p g k a")
                    .broadcast_to([P, NG, 4, HD])).then_inc(pool_r, 1)

            pipeline(pool, [(0, spread)], NT, 4, 4)

            def rotate(t, j):
                pool.wait_ge(a_tq, 2 * t + 2)
                wait_reuse(pool, a_s, t - 3)
                nc.gpsimd.tensor_tensor(QKR[:, j, :, :], TQ[:, j, 0::2, :], TQ[:, j, 1::2, :], ALU.add)\
                    .then_inc(a_qk, 1)

            def spread_queries(t, j):
                pool.wait_ge(a_qk, t + 1)
                nc.gpsimd.tensor_tensor(
                    QD[:, j, :, :, :],
                    QKR[:, j, 0, :].rearrange("p (b a q) -> p b a q", b=BT, a=1).broadcast_to([P, BT, 4, SQ]),
                    headmask[:, :].rearrange("p (a h c) -> p a h c", a=1, c=1).broadcast_to([P, BT, 4, SQ]),
                    ALU.mult).then_inc(a_qd, 1)

            def normalise_probs(t, j):
                pool.wait_ge(a_inv, t + 1)
                nc.gpsimd.tensor_tensor(
                    SX[:, j, :, :], SX[:, j, :, :],
                    sinv[:, j, :].rearrange("p (n a) -> p n a", a=1).broadcast_to([P, 16, SQ]),
                    ALU.mult).then_inc(a_pn, 1)

            pipeline(pool, [(2, rotate), (4, normalise_probs), (2, spread_queries)], NT, 4, 6)


        @block.tensor
        def _(pe):
            pe.wait_ge(ld_w, NW)
            mm(psum[4][0:1, 0:P], bias[:, 2:3], wo_s[:, :]).then_inc(brow_pe, 1)
            pe.wait_ge(ones_ok, 1)
            pe.wait_ge(brow_ok, 1)
            mm(psum[5][:, 0:P], ones1[0:1, :], brow[0:1, :]).then_inc(brow_all, 1)

            def turn_norm(u, h):
                wait_reuse(pe, n0_xt, u - 1)
                for j in range(4):
                    pe.wait_ge(n0_xn, 4 * u + (j + 1))
                    last = tr(psum[h][:, j * P:(j + 1) * P], xn[:, h, j, :])
                last.then_inc(n0_tr, 1)

            def queries(u, h):
                pe.wait_ge(n0_xt, u + 1)
                wait_reuse(pe, n0_qt, u - 1)
                mm(psum[2 + h][:, :], wq_s[:, :], xg[:, h, :]).then_inc(n0_q, 1)

            pipeline(pe, [(0, turn_norm), (1, queries)], NT // 4, 2, 2)

            def ctx_transpose(n, i, b, first):
                pe.wait_ge(ld_ctx[b % BT], 32 * i + 32)
                if not first:
                    pe.wait_ge(ev_w, n)
                for j in range(KC):
                    tr(psum[0][:, j * P:(j + 1) * P], CX[:, b % BT, j, :])
                tr(psum[0][:, KC * P:S2], CXE[0:1, b % BT, :], 1).then_inc(pe_l, 1)

            def keys(n, b, first):
                pe.wait_ge(ev_l, n + 1)
                if not first:
                    pe.wait_ge(ev_k, n)
                wait_reuse(pe, ev_e, n - 2)
                mm(psum[1][:, 0:S2], wk_s[:, :], CT[:, b % 2, :]).then_inc(pe_k, 1)

            def values(n, b):
                pe.wait_ge(ev_l, n + 1)
                for j in range(KC):
                    mm(psum[0][:, j * P:(j + 1) * P], CT[:, b % 2, j * P:(j + 1) * P], wv_s[:, :])
                mm(psum[0][0:4, KC * P:KC * P + P], CT[:, b % 2, KC * P:S2].broadcast_to([P, 4]), wv_s[:, :])\
                    .then_inc(pe_v, 1)

            def energy(n, b, g, first):
                if g == 0:
                    pe.wait_ge(ev_k, n + 1)
                    pe.wait_ge(pool_q, n + 1)
                if not (first and g < 2):
                    pe.wait_ge(dve_min, 4 * n + (g - 1))
                mm(psum[2 + g % 2][:, 0:S2], QB[:, b, 4 * g:4 * g + 4, :].rearrange("p h q -> p (h q)"),
                   KT[:, b % 2, :]).then_inc(pe_s, 1)

            def turn(m, b, g, first):
                pe.wait_ge(act_exp, 4 * m + (g + 1))
                if not (first and g < 2):
                    pe.wait_ge(ev_t, 4 * m + (g - 1))
                bank = psum[4 + g % 2]
                for j in range(KC):
                    last = tr(bank[:, j * P:(j + 1) * P], PR[:, b % 2, g, j * P:(j + 1) * P])
                last.then_inc(pe_t, 1)

            def turn_last_key(m, b, more):
                pe.wait_ge(act_exp, 4 * m + 4)
                if more:
                    pe.wait_ge(ev_k, m + 3)
                tr(psum[1][0:4, 3 * P:4 * P], PR[:, b % 2, :, KC * P]).then_inc(pe_e, 1)

            def attend(m, b, g):
                pe.wait_ge(ev_t, 4 * m + (g + 1))
                if g == 0:
                    pe.wait_ge(ev_w, m + 1)
                col = (b % 2) * P
                for j in range(KC):
                    last = mm(psum[6 + b // 2][32 * g:32 * g + 32, col:col + P],
                              VT[:, b, j * P + 32 * g:j * P + 32 * g + 32],
                              PT[:, g % 2, j * P:(j + 1) * P], start=(j == 0), stop=False)
                last.then_inc(pe_a, 1)

            def attend_last_key(m, b):
                pe.wait_ge(ev_e, m + 1)
                pe.wait_ge(ev_v, m + 1)
                col = (b % 2) * P
                mm(psum[6 + b // 2][:, col:col + P], VE[:, b, :], PTE[:, b % 2, :], start=False)\
                    .then_inc(pe_o, 1)

            def step(i, b, more, first_tile):
                n = i * BT + b
                m, pb = n - 1, (b - 1) % BT
                prev = not first_tile or b >= 1
                nb, ni = (b + 1) % BT, i + (b + 1) // BT
                energy(n, b, 0, first_tile and b == 0)
                if prev:
                    turn(m, pb, 0, first_tile and b == 1)
                if not first_tile or b >= 2:
                    attend(n - 2, (b - 2) % BT, 3)
                    attend_last_key(n - 2, (b - 2) % BT)
                if more:
                    ctx_transpose(n + 1, ni, nb, False)
                energy(n, b, 1, first_tile and b == 0)
                if prev:
                    turn(m, pb, 1, first_tile and b == 1)
                if more:
                    keys(n + 1, nb, False)
                if prev:
                    if pb % 2 == 0 and not first_tile:
                        pe.wait_ge(ev_o, i * 2 + (b - 1) // 2 - 1)
                    attend(m, pb, 0)
                energy(n, b, 2, False)
                if prev:
                    turn(m, pb, 2, False)
                    attend(m, pb, 1)
                if more:
                    values(n + 1, nb)
                energy(n, b, 3, False)
                if prev:
                    turn_last_key(m, pb, more)
                    turn(m, pb, 3, False)
                    attend(m, pb, 2)

            pe.wait_ge(n0_qt, NT // 4)
            ctx_transpose(0, 0, 0, True)
            keys(0, 0, True)
            values(0, 0)
            for b in range(BT):
                step(0, b, True, True)
            with pe.Fori(1, NT - 1) as i:
                for b in range(BT):
                    step(i, b, True, False)
            for b in range(BT):
                step(NT - 1, b, b < BT - 1, False)
            m = NB - 1
            turn(m, BT - 1, 0, False)
            attend(m - 1, BT - 2, 3)
            attend_last_key(m - 1, BT - 2)
            turn(m, BT - 1, 1, False)
            attend(m, BT - 1, 0)
            turn(m, BT - 1, 2, False)
            attend(m, BT - 1, 1)
            pe.wait_ge(ev_e, m)
            turn_last_key(m, BT - 1, False)
            turn(m, BT - 1, 3, False)
            attend(m, BT - 1, 2)
            attend(m, BT - 1, 3)
            attend_last_key(m, BT - 1)

            pe.wait_ge(ev_t, 4 * NB)
            pe.wait_ge(act_exp, 4 * NB)
            for k in range(4):
                for b in range(BT):
                    last = mm(psum[k][32 * b:32 * b + 32, 0:NT * NG],
                              ident[32 * k:32 * k + 32, 32 * k:32 * k + 32],
                              RSUM[32 * k:32 * k + 32, :, b, :])
            last.then_inc(pe_rs, 1)
            pe.wait_ge(dve_rs, 1)
            pe.wait_ge(ev_o, NB // 2)

            def turn_inverse(t, j):
                pe.wait_ge(pool_r, t + 1)
                wait_reuse(pe, dve_otn, t - 3)
                tr(psum[j][:, 0:P], RIE[:, j, :]).then_inc(pe_r, 1)

            def out_project(t, j):
                pe.wait_ge(dve_otn, t + 1)
                wait_reuse(pe, dve_x1, t - 3)
                mm(psum[4 + j][:, 0:P], OTN[:, j, :], wo_s[:, :]).then_inc(pe_x1, 1)

            pipeline(pe, [(0, turn_inverse), (1, out_project)], NT, 4, 4)

            pe.wait_ge(wqk_ok, 1)
            pe.wait_ge(dve_x1, NT)

            def turn_x(t, j):
                pe.wait_ge(a_xn, t + 1)
                wait_reuse(pe, a_xt, t)
                tr(psum[0][:, 0:P], xn[:, 0, j, :]).then_inc(a_tr, 1)

            def project(t, j):
                pe.wait_ge(a_xt, t + 1)
                wait_reuse(pe, a_tq, 2 * t - 2)
                for w in range(4):
                    last = mm(psum[2 + j % 2][:, w * P:(w + 1) * P], wqk[:, w, :], xt[:, j, :])
                last.then_inc(a_p, 1)

            def self_values(t, j):
                wait_reuse(pe, a_vb, t)
                for b in range(BT):
                    for g in range(4):
                        last = mm(psum[1][32 * g:32 * g + 32, 32 * b:32 * b + 32],
                                  xt[:, j, b * SQ:(b + 1) * SQ], sw_v[:, :])
                last.then_inc(a_v, 1)

            def scores(t, j):
                pe.wait_ge(a_kb, t + 1)
                pe.wait_ge(a_qd, t + 1)
                wait_reuse(pe, a_sx, t - 1)
                for b in range(BT):
                    last = mm(psum[4 + j % 2][:, b * P:(b + 1) * P],
                              QD[:, j, b, :, :].rearrange("p h q -> p (h q)"),
                              KB[:, j, b, :, :].rearrange("p h q -> p (h q)"))
                last.then_inc(a_s, 1)

            def turn_probs(t, j):
                pe.wait_ge(a_pn, t + 1)
                wait_reuse(pe, a_sp, t)
                for b in range(BT):
                    last = tr(psum[6][:, b * P:(b + 1) * P],
                              SX[:, j, 4 * b:4 * b + 4, :].rearrange("p n k -> p (n k)"))
                last.then_inc(a_pt, 1)

            def weigh_values(t, j):
                pe.wait_ge(a_sp, t + 1)
                pe.wait_ge(a_vb, t + 1)
                wait_reuse(pe, a_x2, t)
                for b in range(BT):
                    for g in range(4):
                        last = mm(psum[7][32 * g:32 * g + 32, b * SQ:(b + 1) * SQ],
                                  VB[:, j, b, :, :].rearrange("p h d -> p (h d)"),
                                  SP[:, j, b, g * SQ:(g + 1) * SQ])
                last.then_inc(a_o, 1)

            def project_out(t, j):
                pe.wait_ge(a_so, t + 1)
                mm(psum[7][:, P:2 * P], SO[:, j, :], sw_o[:, :]).then_inc(a_wo, 1)

            pipeline(pe, [(6, project_out), (0, turn_x), (3, scores), (1, project), (5, weigh_values),
                          (1, self_values), (4, turn_probs)], NT, 4, 6)

            pe.wait_ge(a_x2, NT)

            def turn_router(u, h):
                wait_reuse(pe, r_xtt, u - 1)
                for j in range(4):
                    pe.wait_ge(r_xn, 4 * u + (j + 1))
                    last = tr(psum[h][:, j * P:(j + 1) * P], xn[:, h, j, :])
                last.then_inc(r_tr, 1)

            def logits(u, h):
                pe.wait_ge(r_xt, u + 1)
                wait_reuse(pe, r_cp, u - 1)
                for j in range(4):
                    last = mm(psum[2 + h][:, j * E:(j + 1) * E], xg[:, h, j * P:(j + 1) * P], wg_s[:, :])
                last.then_inc(r_lg, 1)

            pipeline(pe, [(0, turn_router), (1, logits)], NT // 4, 2, 2)

            pe.wait_ge(t_dve, 1)
            for a in range(HALVES):
                last = tr(psum[0][:, a * P:(a + 1) * P],
                          PRB[:, a * 16:(a + 1) * 16, :].rearrange("p i e -> p (i e)"))
            last.then_inc(t_pe, 1)
            for k in range(len(bits)):
                pe.wait_ge(t_dve, 2 + k)
                mm(psum[1][:, 0:1], same[:, :], cnt[:, :]).then_inc(t_pe, 1)
            nb = len(bits)
            pe.wait_ge(t_dve, 2 + nb)
            mm(psum[2][:, 0:1], same[:, :], cnt[:, :]).then_inc(t_pe, 1)
            pe.wait_ge(t_dve, 3 + nb)
            for a in range(HALVES):
                for c in range(a + 1):
                    last = mm(psum[3][:, a:a + 1], earlier[:, :] if c == a else same[:, :], tot[:, c:c + 1],
                              start=(c == 0), stop=(c == a))
            last.then_inc(t_pe, 1)
            pe.wait_ge(t_dve, 4 + nb)
            for a in range(HALVES):
                last = tr(psum[0][:, a * P:(a + 1) * P], GT[:, a, :])
            last.then_inc(t_pe, 1)

            pe.wait_ge(ld_ffn, 32)
            pe.wait_ge(r_xtt, NT // 4)
            pe.wait_ge(t_done, 1)

            def hidden(i, e, wait):
                for j in range(FC):
                    if wait:
                        pe.wait_ge(f_g, i * (E * FC) + ((e - 2) * FC + j + 1))
                    mm(psum[2 * (e % 2) + j][:, :], w1_s[:, e, j * P:(j + 1) * P],
                       XTT[:, bass.ds(i * 512, 512)]).then_inc(f_h, 1)

            def expand(i, e, wait):
                pe.wait_ge(f_g, i * (E * FC) + (e * FC + FC))
                if wait:
                    pe.wait_ge(f_x, i * (4 * E) + (4 * (e - 2) + 4))
                for t in range(4):
                    for j in range(FC):
                        last = mm(psum[4 + e % 2][:, t * P:(t + 1) * P], HT[:, e % 2, j, t * P:(t + 1) * P],
                                  w2_s[:, e, j, :], start=(j == 0), stop=(j == FC - 1))
                last.then_inc(f_y, 1)

            with pe.Fori(0, NT // 4) as i:
                hidden(i, 0, False)
                for e in range(E):
                    if e + 1 < E:
                        hidden(i, e + 1, e + 1 >= 2)
                    expand(i, e, e >= 2)
                pe.wait_ge(f_x, i * (4 * E) + 4 * E)

        @block.vector
        def _(dve):
            V = nc.vector
            chain = [0]

            def link(ins):
                chain[0] += 1
                ins.then_inc(dve_c, 1)
                dve.wait_ge(dve_c, chain[0])

            def moments_to_rstd(st_sem, rs_sem, done=None):
                me, mo = stats[:, :, 1], stats[:, :, 4]
                link(V.tensor_tensor(mv[:, :, 0], me, mo, ALU.add))
                link(V.tensor_scalar(mv[:, :, 0], mv[:, :, 0], 0.5, None, ALU.mult))
                link(V.tensor_tensor(mv[:, :, 1], me, mv[:, :, 0], ALU.subtract))
                link(V.tensor_tensor(mv[:, :, 1], mv[:, :, 1], mv[:, :, 1], ALU.mult))
                link(V.tensor_tensor(std[:, :], stats[:, :, 2], stats[:, :, 5], ALU.add))
                link(V.tensor_scalar(std[:, :], std[:, :], 1.0 / D, EPS, ALU.mult, ALU.add))
                V.tensor_tensor(std[:, :], std[:, :], mv[:, :, 1], ALU.add).then_inc(st_sem, 1)
                dve.wait_ge(rs_sem, 1)
                link(V.reciprocal(rstd[:, :], std[:, :]))
                link(V.tensor_tensor(shift[:, :], mv[:, :, 0], rstd[:, :], ALU.mult))
                last = V.tensor_scalar(shift[:, :], shift[:, :], -1.0, None, ALU.mult)
                if done is not None:
                    last.then_inc(done, 1)

            def normalise(dst, src, tile):
                return V.tensor_scalar(dst, src,
                                       mv[:, bass.ds(tile, 1), 0], rstd[:, bass.ds(tile, 1)],
                                       ALU.subtract, ALU.mult)

            link(V.memset(thr[:, :], 0))
            for q in range(NLX):
                dve.wait_ge(ld_x[q], 16)
                with dve.Fori(q * NT // (4 * NLX), (q + 1) * NT // (4 * NLX)) as i:
                    for j in range(4):
                        V.bn_stats(stats[:, bass.ds(i * 4 + j, 1), :].rearrange("p a s -> p (a s)"),
                                   X[:, bass.ds(i * 4 + j, 1), :].rearrange("p a c -> p (a c)"))\
                            .then_inc(dve_st1, 1)
            dve.wait_ge(dve_st1, NT)
            moments_to_rstd(n0_std, n0_rstd)
            dve.wait_ge(ld_w, NW)
            V.tensor_scalar(qbias[:, :], bias[:, 0:1], -SCALE, None, ALU.mult).then_inc(n0_bias, 1)
            dve.wait_ge(brow_pe, 1)
            V.tensor_tensor(brow[:, :], brow[:, :], psum[4][0:1, 0:P], ALU.add).then_inc(brow_ok, 1)

            def norm_queries(u, h):
                wait_reuse(dve, n0_tr, u - 1)
                for j in range(4):
                    t = u * 4 + j
                    normalise(xn[:, h, j, :], X[:, bass.ds(t, 1), :].rearrange("p a c -> p (a c)"), t)\
                        .then_inc(n0_xn, 1)

            pipeline(dve, [(0, norm_queries)], NT // 4, 2, 2)
            dve.wait_ge(brow_all, 1)
            V.tensor_copy(BROW[:, :], psum[5][:, 0:P]).then_inc(brow_sp, 1)
            qv = sw_q[:, :].rearrange("p (h a f) -> p h a f", h=NG * 4, a=2)
            kv = sw_k[:, :].rearrange("p (k g a f) -> p k g a f", k=NG, g=1, a=2)
            for a in range(2):
                for w, s in ((0, a), (1, 1 - a)):
                    V.tensor_copy(wqk[:, w, :].rearrange("p (h a f) -> p h a f", h=NG * 4, a=2)[:, :, a, :],
                                  qv[:, :, s, :])
                    last = V.tensor_copy(
                        wqk[:, 2 + w, :].rearrange("p (k g a f) -> p k g a f", k=NG, g=4, a=2)[:, :, :, a, :],
                        kv[:, :, :, s, :].broadcast_to([P, NG, 4, 4]))
            last.then_inc(wqk_ok, 1)

            def mask_min(n, b, g, first):
                dve.wait_ge(pe_s, 4 * n + (g + 1))
                if g == 0:
                    dve.wait_ge(pool_m, n + 1)
                if not first:
                    dve.wait_ge(act_exp, 4 * n + (g - 3))
                V.memset(waited[:, g:g + 1], 0.0)
                V.tensor_tensor_reduce(SM[:, g, :], psum[2 + g % 2][:, 0:S2], MB[:, b, :], 1.0, float(3e38),
                                       ALU.add, ALU.min, MN[:, g:g + 1]).then_inc(dve_min, 1)

            def evac_turned(m, b, g, first):
                dve.wait_ge(pe_t, 4 * m + (g + 1))
                if not (first and g < 2):
                    dve.wait_ge(pe_a, 4 * m + (g - 1))
                V.tensor_copy(PT[:, g % 2, :], psum[4 + g % 2][:, 0:KC * P]).then_inc(ev_t, 1)

            def batch(i, b, prev, more, first_tile):
                n = i * BT + b
                m, pb = n - 1, (b - 1) % BT
                mask_min(n, b, 0, first_tile and b == 0)
                if prev:
                    evac_turned(m, pb, 0, first_tile and b == 1)
                mask_min(n, b, 1, first_tile and b == 0)
                if prev:
                    evac_turned(m, pb, 1, first_tile and b == 1)
                mask_min(n, b, 2, first_tile and b == 0)
                if prev:
                    evac_turned(m, pb, 2, False)
                mask_min(n, b, 3, first_tile and b == 0)
                if prev:
                    evac_turned(m, pb, 3, False)

            for b in range(BT):
                batch(0, b, b > 0, True, True)
            with dve.Fori(1, NT - 1) as i:
                for b in range(BT):
                    batch(i, b, True, True, False)
            for b in range(BT):
                batch(NT - 1, b, True, b < BT - 1, False)
            for g in range(NG):
                evac_turned(NB - 1, BT - 1, g, False)

            dve.wait_ge(pe_rs, 1)
            for k in range(4):
                last = V.reciprocal(RIN[:, k, :, :].rearrange("p i g -> p (i g)"), psum[k][:, 0:NT * NG])
            last.then_inc(dve_rs, 1)
            dve.wait_ge(pool_o, NB // 2)
            dve.wait_ge(x_biased, 1)

            def normalise_out(t, j):
                dve.wait_ge(pe_r, t + 1)
                wait_reuse(dve, pe_x1, t - 3)
                V.tensor_tensor(OTN[:, j, :], OT[:, bass.ds(t * P, P)], psum[j][:, 0:P],
                                ALU.mult).then_inc(dve_otn, 1)

            def cross_residual(t, j):
                dve.wait_ge(pe_x1, t + 1)
                xi = X[:, bass.ds(t, 1), :].rearrange("p a c -> p (a c)")
                V.tensor_tensor(xi, xi, psum[4 + j][:, 0:P], ALU.add).then_inc(dve_x1, 1)

            def cross_statistics(t, j):
                dve.wait_ge(dve_x1, t + 1)
                V.bn_stats(stats[:, bass.ds(t, 1), :].rearrange("p a s -> p (a s)"),
                           X[:, bass.ds(t, 1), :].rearrange("p a c -> p (a c)")).then_inc(dve_st1, 1)

            pipeline(dve, [(0, normalise_out), (2, cross_residual), (3, cross_statistics)], NT, 4, 4)
            dve.wait_ge(dve_st1, 2 * NT)
            moments_to_rstd(n1_std, n1_rstd, n1_shift)

            def rotary(t, j):
                dve.wait_ge(a_p, t + 1)
                wait_reuse(dve, a_qk, t - 3)
                for w in range(2):
                    V.tensor_tensor(
                        TQ[:, j, w::2, :].rearrange("p w (b s) -> p w b s", b=BT),
                        psum[2 + j % 2][:, :].rearrange("p (w b s) -> p w b s", w=4, b=BT)[:, w::2],
                        rope[:, w, :].rearrange("p (c d s) -> p c d s", c=1, d=1)
                        .broadcast_to([P, 2, BT, SQ]), ALU.mult).then_inc(a_tq, 1)

            def shift_scores(t, j):
                dve.wait_ge(a_s, t + 1)
                V.tensor_reduce(smx[:, j, :], psum[4 + j % 2][:, :].rearrange("p (n k) -> p n k", n=16), AX_X,
                                ALU.max).then_inc(a_mx, 1)
                wait_reuse(dve, a_pt, t - 3)
                dve.wait_ge(a_mx, t + 1)
                V.tensor_tensor(SX[:, j, :, :], psum[4 + j % 2][:, :].rearrange("p (n k) -> p n k", n=16),
                                smx[:, j, :].rearrange("p (n a) -> p n a", a=1).broadcast_to([P, 16, SQ]),
                                ALU.subtract).then_inc(a_sx, 1)

            def sum_probs(t, j):
                dve.wait_ge(a_ex, t + 1)
                V.tensor_reduce(ssum[:, j, :], SX[:, j, :, :], AX_X, ALU.add).then_inc(a_sum, 1)

            def invert_sums(t, j):
                dve.wait_ge(a_sum, t + 1)
                V.reciprocal(sinv[:, j, :], ssum[:, j, :]).then_inc(a_inv, 1)

            def residual(t, j):
                dve.wait_ge(a_wo, t + 1)
                xi = X[:, bass.ds(t, 1), :].rearrange("p a c -> p (a c)")
                V.tensor_tensor(xi, xi, psum[7][:, P:2 * P], ALU.add).then_inc(a_x2, 1)

            def statistics(t, j):
                dve.wait_ge(a_x2, t + 1)
                V.bn_stats(stats[:, bass.ds(t, 1), :].rearrange("p a s -> p (a s)"),
                           X[:, bass.ds(t, 1), :].rearrange("p a c -> p (a c)")).then_inc(a_st, 1)

            pipeline(dve, [(4, sum_probs), (6, residual), (4, invert_sums), (3, shift_scores), (6, statistics),
                           (1, rotary)], NT, 4, 6)
            dve.wait_ge(a_st, NT)
            moments_to_rstd(n2_std, n2_rstd)

            def norm_router(u, h):
                wait_reuse(dve, r_tr, u - 1)
                for j in range(4):
                    t = u * 4 + j
                    normalise(xn[:, h, j, :], X[:, bass.ds(t, 1), :].rearrange("p a c -> p (a c)"), t)\
                        .then_inc(r_xn, 1)

            def keep_logits(u, h):
                dve.wait_ge(r_lg, u + 1)
                V.tensor_copy(PRB[:, bass.ds(u * 4, 4), :].rearrange("p i e -> p (i e)"),
                              psum[2 + h][:, 0:4 * E]).then_inc(r_cp, 1)

            pipeline(dve, [(0, norm_router), (2, keep_logits)], NT // 4, 2, 2)
            dve.wait_ge(r_cp, NT // 4)

            def over_experts(v):
                return v.rearrange("p (i a) -> p i a", a=1).broadcast_to([P, NT, E])

            link(V.tensor_reduce(rmx[:, :], PRB[:, :, :], AX_X, ALU.max))
            V.tensor_tensor(PRB[:, :, :], PRB[:, :, :], over_experts(rmx[:, :]), ALU.subtract).then_inc(t_act, 1)
            dve.wait_ge(t_exp, 1)
            link(V.tensor_reduce(rmx[:, :], PRB[:, :, :], AX_X, ALU.add))
            link(V.reciprocal(any_[:, :], rmx[:, :]))
            V.tensor_tensor(PRB[:, :, :], PRB[:, :, :], over_experts(any_[:, :]), ALU.mult).then_inc(t_dve, 1)
            dve.wait_ge(t_pe, 1)
            link(V.tensor_copy(PRT[:, :, :].rearrange("p a t -> p (a t)"), psum[0][:, 0:HALVES * P]))
            prt = PRT[:, :, :].rearrange("p a t -> p (a t)")
            cmpf = cmp_[:, :, :].rearrange("p a t -> p (a t)")

            for k, bit in enumerate(bits):
                link(V.tensor_scalar(thr_try[:, :], thr[:, :], 1 << bit, None, ALU.bitwise_or))
                V.tensor_scalar(cmpf, prt, thr_try[:, :].bitcast(F32), 0.0, ALU.is_ge, ALU.add,
                                accum_out=cnt[:, :]).then_inc(t_dve, 1)
                dve.wait_ge(t_pe, 2 + k)
                link(V.tensor_scalar(bit_ok[:, :], psum[1][:, 0:1], CAP - 0.5, float(1 << bit),
                                     ALU.is_ge, ALU.mult))
                link(V.tensor_tensor(thr[:, :], thr[:, :], bit_ok[:, :], ALU.bitwise_or))
            nb = len(bits)
            thf = thr[:, :].bitcast(F32)
            V.tensor_scalar(GT[:, :, :].rearrange("p a t -> p (a t)"), prt, thf, 0.0, ALU.is_gt, ALU.add,
                            accum_out=cnt[:, :]).then_inc(t_dve, 1)
            dve.wait_ge(t_pe, 2 + nb)
            link(V.tensor_scalar(need[:, 0:1], psum[2][:, 0:1], -1.0, float(CAP), ALU.mult, ALU.add))
            for a in range(HALVES):
                link(V.tensor_scalar(EQ[:, a, :], PRT[:, a, :], thf, 0.0, ALU.is_equal, ALU.add,
                                     accum_out=tot[:, a:a + 1]))
            V.memset(cmpf, 0.0).then_inc(t_dve, 1)
            dve.wait_ge(t_pe, 3 + nb)
            link(V.tensor_copy(need[:, 1:2], need[:, 0:1]))
            link(V.tensor_tensor(need[:, :], need[:, :], psum[3][:, 0:HALVES], ALU.subtract))
            for a in range(HALVES):
                link(V.tensor_tensor_scan(PFX[:, a, :], EQ[:, a, :], zero_row[:, :], 0.0, ALU.add, ALU.add))
                link(V.tensor_scalar(PFX[:, a, :], PFX[:, a, :], need[:, a:a + 1], None, ALU.is_le))
            link(V.tensor_tensor(PFX[:, :, :], PFX[:, :, :], EQ[:, :, :], ALU.mult))
            V.tensor_tensor(GT[:, :, :], GT[:, :, :], PFX[:, :, :], ALU.add).then_inc(t_dve, 1)
            dve.wait_ge(t_pe, 4 + nb)
            link(V.tensor_copy(SEL[:, :, :].rearrange("p i e -> p (i e)"), psum[0][:, 0:HALVES * P]))
            link(V.tensor_tensor(KEY[:, :, :], PRB[:, :, :], SEL[:, :, :], ALU.mult))
            link(V.tensor_scalar(RT[:, :, :], SEL[:, :, :], -1.0, None, ALU.add))
            link(V.tensor_tensor(KEY[:, :, :], KEY[:, :, :], RT[:, :, :], ALU.add))
            link(V.tensor_reduce(any_[:, :], KEY[:, :, :], AX_X, ALU.max))
            link(V.tensor_scalar(rmx[:, :], any_[:, :], 0.0, None, ALU.is_lt))
            link(V.tensor_scalar(any_[:, :], any_[:, :], 0.0, None, ALU.is_ge))
            link(V.tensor_tensor(KEY[:, :, :], KEY[:, :, :], over_experts(any_[:, :]), ALU.mult))
            link(V.tensor_tensor(RT[:, :, :], PRB[:, :, :], over_experts(rmx[:, :]), ALU.mult))
            link(V.tensor_tensor(KEY[:, :, :], KEY[:, :, :], RT[:, :, :], ALU.add))
            link(V.tensor_reduce(rmx[:, :], KEY[:, :, :], AX_X, ALU.max))
            link(V.tensor_tensor(KEY[:, :, :], KEY[:, :, :], over_experts(rmx[:, :]), ALU.is_equal))
            by_rank = rank[:, :].rearrange("p (a e) -> p a e", a=1).broadcast_to([P, NT, E])
            link(V.tensor_tensor(KEY[:, :, :], KEY[:, :, :], by_rank, ALU.mult))
            link(V.tensor_reduce(rmx[:, :], KEY[:, :, :], AX_X, ALU.max))
            link(V.tensor_tensor(KEY[:, :, :], by_rank, over_experts(rmx[:, :]), ALU.is_equal))
            V.tensor_tensor(GATE[:, :, :], KEY[:, :, :], PRB[:, :, :], ALU.mult).then_inc(t_done, 1)
            dve.wait_ge(t_done, 1)

            with dve.Fori(0, NT // 4) as i:
                for e in range(E):
                    dve.wait_ge(f_y, i * E + (e + 1))
                    if e:
                        dve.wait_ge(f_x, i * (4 * E) + 4 * e)
                    for t in range(4):
                        xi = X[:, bass.ds(i * 4 + t, 1), :].rearrange("p a c -> p (a c)")
                        V.scalar_tensor_tensor(xi, psum[4 + e % 2][:, t * P:(t + 1) * P],
                                               GATE[:, bass.ds(i * 4 + t, 1), e], xi, ALU.mult, ALU.add)\
                            .then_inc(f_x, 1)


_INS = ["x", "ctx_1024", "mask_BxSxS2_ik1", "L0_xattn_Wq", "L0_xattn_bq", "L0_xattn_Wk", "L0_xattn_bk",
        "L0_xattn_Wv", "L0_xattn_bv", "L0_xattn_Wo", "L0_xattn_bo", "L0_attn_w_q", "L0_attn_w_k",
        "L0_attn_w_v", "L0_attn_w_o", "L0_ffn_Wg", "L0_ffn_W1", "L0_ffn_W2"]


def kernel(**inputs):
    import concourse.bacc as bacc
    from concourse.bass_utils import run_bass_kernel_spmd

    nc = bacc.Bacc("TRN2", target_bir_lowering=False, num_devices=1)
    arrays, args = {}, []
    for name in _INS:
        a = np.ascontiguousarray(inputs[name])
        arrays["in_" + name] = a
        args.append(nc.dram_tensor("in_" + name, a.shape, mybir.dt.from_np(a.dtype), kind="ExternalInput").ap())
    B, S, D = inputs["x"].shape
    table = shape_constants(B, S)
    for name in _CONSTS:
        a = np.ascontiguousarray(table[name])
        arrays["const_" + name] = a
        args.append(nc.dram_tensor("const_" + name, a.shape, F32, kind="ExternalInput").ap())
    args.append(nc.dram_tensor("out", (B, S, D), F32, kind="ExternalOutput").ap())
    perceiver_block(nc, *args)
    r = run_bass_kernel_spmd(nc, [arrays], core_ids=[0])
    return r.results[0]["out"]
```

```python
from contextlib import ExitStack

import numpy as np

import concourse.bass as bass
from concourse import mybir

F32 = mybir.dt.float32
I32 = mybir.dt.int32
F32R = mybir.dt.float32r
ALU = mybir.AluOpType
ACT = mybir.ActivationFunctionType
AX_X = mybir.AxisListType.X

P = 128
HD = 8
NG = 4
SQ = 32
BT = P // SQ
BIG = float(2.0 ** 100)
EPS = 1e-5


def shape_constants(B, S):
    c = np.arange(P)
    one = np.float32
    out = {}
    out["ident"] = np.eye(P, dtype=one)
    out["headmask"] = (((c % 32) // HD)[:, None] == np.arange(4)[None, :]).astype(one)
    f = (c % HD) % 4
    inv = (1.0 / np.float32(10000.0) ** (np.arange(4, dtype=one) * 2.0 / HD)).astype(one)
    ang = (np.arange(S, dtype=one)[None, :] * inv[f][:, None]).astype(one)
    sign = np.where(c % HD < 4, -1.0, 1.0).astype(one)[:, None]
    out["rope"] = np.concatenate([np.cos(ang), np.sin(ang) * sign], axis=1).astype(one)
    e, t = c % 8, c // 8
    same = e[:, None] == e[None, :]
    out["same_expert"] = same.astype(one)
    out["earlier_tile"] = (same & (t[:, None] < t[None, :])).astype(one)
    out["rank"] = np.broadcast_to(8.0 - np.arange(8), (P, 8)).astype(one).copy()
    return out


_CONSTS = ["ident", "headmask", "rope", "same_expert", "earlier_tile", "rank"]


def perceiver_block(nc, x, ctx_in, mask, Wq, bq, Wk, bk, Wv, bv, Wo, bo,
                    w_q, w_k, w_v, w_o, Wg, W1, W2,
                    c_ident, c_head, c_rope, c_same, c_earlier, c_rank, out):
    NB, S, D = x.shape
    S2 = ctx_in.shape[1]
    T = NB * S
    NT = T // P
    KC = (S2 - 1) // P
    E, F = Wg.shape[1], W1.shape[2]
    FC = F // P
    CAP = max(1, T // E)
    assert (D, S, NB % BT, S2 - KC * P, E) == (P, SQ, 0, 1, 8)
    SCALE = 1.0 / float(np.sqrt(np.float32(HD)))
    HALVES = NT // 16

    with ExitStack() as ctx:
        def sb(name, shape, dt=F32):
            return ctx.enter_context(nc.sbuf_tensor(name, shape, dt))

        def sem(name):
            return ctx.enter_context(nc.semaphore(name))

        psum = [ctx.enter_context(nc.psum_tensor(f"bank{i}", [P, 512], F32)) for i in range(8)]

        ident = sb("ident", [P, P])
        headmask = sb("headmask", [P, 4])
        rope = sb("rope", [P, 2, S])
        same = sb("same", [P, P])
        earlier = sb("earlier", [P, P])
        rank = sb("rank", [P, 8])
        wq_s = sb("wq_s", [P, P])
        wk_s = sb("wk_s", [P, P])
        wv_s = sb("wv_s", [P, P])
        wo_s = sb("wo_s", [P, P])
        bias = sb("bias", [P, 3])
        brow = sb("brow", [1, P])
        BROW = sb("BROW", [P, P])
        qbias = sb("qbias", [P, 1])
        ones1 = sb("ones1", [1, P])
        sw_q = sb("sw_q", [P, P])
        sw_k = sb("sw_k", [P, NG * HD])
        sw_v = sb("sw_v", [P, NG * HD])
        sw_o = sb("sw_o", [P, P])
        wqk = sb("wqk", [P, 4, P])
        wg_s = sb("wg_s", [P, E])
        w1_s = sb("w1_s", [P, E, F])
        w2_s = sb("w2_s", [P, E, FC, P])

        X = sb("X", [P, NT, P])
        QT = sb("QT", [P, T])
        OT = sb("OT", [P, T])
        stats = sb("stats", [P, NT, 6])
        mv = sb("mv", [P, NT, 2])
        std = sb("std", [P, NT])
        rstd = sb("rstd", [P, NT])
        shift = sb("shift", [P, NT])
        RSUM = sb("RSUM", [P, NT, BT, NG])
        RIN = sb("RIN", [P, 4, NT, NG])

        xn = sb("xn", [P, 2, 4, P])
        xg = sb("xg", [P, 2, 512])

        cross = ExitStack()

        def sbc(name, shape, dt=F32):
            return cross.enter_context(nc.sbuf_tensor(name, shape, dt))


        CX = sbc("CX", [P, BT, KC, P])
        CXE = sbc("CXE", [1, BT, P])
        MK = sbc("MK", [P, BT, S2], I32)
        MB = sbc("MB", [P, BT, S2])
        CT = sbc("CT", [P, 2, S2])
        SE = S2 + S2 % 2
        KH = sbc("KH", [P, 2, SE], F32R)
        KL = sbc("KL", [P, 2, SE], F32R)
        VT = sbc("VT", [P, BT, KC * P])
        VE = sbc("VE", [4, BT, P])
        QB = sbc("QB", [P, 2, 4, SQ])
        QH = sbc("QH", [P, BT, 4, SQ], F32R)
        QL = sbc("QL", [P, BT, 4, SQ], F32R)
        SM = sbc("SM", [P, NG, S2])
        MN = sbc("MN", [P, NG])
        PR = sbc("PR", [P, 2, NG, S2])
        PT = sbc("PT", [P, 2, NG, KC * P])
        PTE = sbc("PTE", [4, 2, P])
        OC = sbc("OC", [P, 2, 2 * P])
        cross.close()

        W1H = sb("W1H", [P, E, F], F32R)
        W1L = sb("W1L", [P, E, F], F32R)
        XH = sb("XH", [P, T], F32R)
        XL = sb("XL", [P, T], F32R)

        xt = sb("xt", [P, 4, P])
        TQ = sb("TQ", [P, 4, 4, P])
        QKR = sb("QKR", [P, 4, 2, P])
        QD = sb("QD", [P, 4, BT, 4, SQ])
        KB = sb("KB", [P, 4, BT, NG, SQ])
        VB = sb("VB", [P, 4, BT, NG, HD])
        SX = sb("SX", [P, 4, 16, SQ])
        smx = sb("smx", [P, 4, 16])
        ssum = sb("ssum", [P, 4, 16])
        sinv = sb("sinv", [P, 4, 16])
        SP = sb("SP", [P, 4, BT, P])
        SO = sb("SO", [P, 4, P])
        RIE = xt
        RTO = xn[:, 0, :, :]
        OTN = SO
        CLAST = xt[:, 0, :]
        CLT = xt[:, 1, :]
        VLM = SO
        v_last = nc.dram_tensor("v_last", (NB, NG, P), F32, kind="Internal").ap()
        assert NB == P

        PRB = sb("PRB", [P, NT, E])
        rmx = sb("rmx", [P, NT])
        PRT = sb("PRT", [P, HALVES, P])
        assert HALVES == 2
        cmp_, GT, EQ, PFX = (QKR[:, k, :, :] for k in range(4))
        cnt = sb("cnt", [P, 1])
        thr = sb("thr", [P, 1], I32)
        thr_next = sb("thr_next", [P, 1], I32)
        bit_off = sb("bit_off", [P, 1], I32)
        tot = sb("tot", [P, 2])
        need = sb("need", [P, 2])
        SEL = sb("SEL", [P, NT, E])
        KEY = sb("KEY", [P, NT, E])
        RT = sb("RT", [P, NT, E])
        any_ = sb("any_", [P, NT])
        GATE = sb("GATE", [P, NT, E])
        HT = [[TQ[:, FC * k + j, :, :].rearrange("p w c -> p (w c)") for j in range(FC)] for k in range(2)]
        LATE = 3
        KEPT = [[OT[:, e * 512:(e + 1) * 512] for e in range(E)],
                [(KB if e < 4 else QD)[:, e % 4, :, :, :].rearrange("p b h q -> p (b h q)") for e in range(E)],
                [(SX if e < 4 else SP)[:, e % 4, :, :].rearrange("p b k -> p (b k)") for e in range(E)]]
        zero_row = sb("zero_row", [P, P])
        warm = sb("warm", [1, 1])
        waited = sb("waited", [1, NG])

        NLX = 4
        ld_x = [sem(f"ld_x{j}") for j in range(NLX)]
        ld_q = sem("ld_q")
        ld_wx = sem("ld_wx")
        ld_s = sem("ld_s")
        ld_ffn = sem("ld_ffn")
        dve_c = sem("dve_c")
        n0_std = sem("n0_std")
        n0_rstd = sem("n0_rstd")
        n0_xn = sem("n0_xn")
        n0_tr = sem("n0_tr")
        n0_xt = sem("n0_xt")
        n0_q = sem("n0_q")
        n0_qt = sem("n0_qt")
        warm_ok = sem("warm_ok")
        x_biased = sem("x_biased")
        brow_all = sem("brow_all")
        brow_sp = sem("brow_sp")
        n0_bias = sem("n0_bias")

        ld_ctx = [sem(f"ld_ctx{b}") for b in range(BT)]
        ld_mask = [sem(f"ld_mask{b}") for b in range(BT)]
        pe_l = sem("pe_l")
        pe_k = sem("pe_k")
        pe_v = sem("pe_v")
        pe_s = sem("pe_s")
        pe_t = sem("pe_t")
        pe_a = sem("pe_a")
        ev_l = sem("ev_l")
        ev_k = sem("ev_k")
        ld_last = sem("ld_last")
        pe_clt = sem("pe_clt")
        dve_clt = sem("dve_clt")
        pe_vl = sem("pe_vl")
        vlm_zero = sem("vlm_zero")
        vlm_ok = sem("vlm_ok")
        st_vl = sem("st_vl")
        ld_ve = [sem(f"ld_ve{b}") for b in range(BT)]
        ev_t = sem("ev_t")
        ev_o = sem("ev_o")
        ev_w = sem("ev_w")
        ev_e = sem("ev_e")
        pe_e = sem("pe_e")
        pe_o = sem("pe_o")
        pool_c = sem("pool_c")
        pool_o = sem("pool_o")
        dve_min = sem("dve_min")
        act_exp = sem("act_exp")
        pool_b = sem("pool_b")
        pool_q = sem("pool_q")
        ev_kl = sem("ev_kl")
        kpad = sem("kpad")
        pool_m = sem("pool_m")

        pe_rs = sem("pe_rs")
        dve_inv = sem("dve_inv")
        dve_rs = sem("dve_rs")
        act_r = sem("act_r")
        act_spread = sem("act_spread")
        pe_r = sem("pe_r")
        pool_otn = sem("pool_otn")
        pe_x1 = sem("pe_x1")
        dve_x1 = sem("dve_x1")
        dve_st1 = sem("dve_st1")
        brow_pe = sem("brow_pe")
        brow_ok = sem("brow_ok")
        n1_std = sem("n1_std")
        n1_rstd = sem("n1_rstd")
        n1_shift = sem("n1_shift")

        a_xn = sem("a_xn")
        a_tr = sem("a_tr")
        a_p = sem("a_p")
        a_v = sem("a_v")
        zero_ok = sem("zero_ok")
        ones_ok = sem("ones_ok")
        a_xt = sem("a_xt")
        a_tq = sem("a_tq")
        a_qk = sem("a_qk")
        a_vb = sem("a_vb")
        a_kb = sem("a_kb")
        a_qd = sem("a_qd")
        a_s = sem("a_s")
        a_mx = sem("a_mx")
        a_sx = sem("a_sx")
        a_ex = sem("a_ex")
        a_sum = sem("a_sum")
        a_inv = sem("a_inv")
        a_pn = sem("a_pn")
        a_pt = sem("a_pt")
        a_sp = sem("a_sp")
        a_o = sem("a_o")
        a_so = sem("a_so")
        a_wo = sem("a_wo")
        a_x2 = sem("a_x2")
        a_st = sem("a_st")
        wqk_ok = sem("wqk_ok")
        n2_std = sem("n2_std")
        n2_rstd = sem("n2_rstd")

        r_xn = sem("r_xn")
        r_tr = sem("r_tr")
        r_xt = sem("r_xt")
        r_xh = sem("r_xh")
        r_xl = sem("r_xl")
        w1_h = sem("w1_h")
        w1_l = sem("w1_l")
        r_lg = sem("r_lg")
        r_cp = sem("r_cp")
        t_act = sem("t_act")
        t_exp = sem("t_exp")
        t_pe = sem("t_pe")
        t_dve = sem("t_dve")
        t_done = sem("t_done")
        f_h = sem("f_h")
        f_g = sem("f_g")
        f_y = sem("f_y")
        f_x = sem("f_x")
        f_keep = sem("f_keep")
        f_late = sem("f_late")
        st_out = sem("st_out")

        block = ctx.enter_context(nc.Block())

        x_tiles = x.rearrange("(i b) s d -> (b s) i d", b=BT)
        out_tiles = out.rearrange("(i b) s d -> (b s) i d", b=BT)
        bits = list(range(29, -1, -1))

        def wait_reuse(eng, s, v):
            if not (isinstance(v, int) and v <= 0):
                eng.wait_ge(s, v)

        def pipeline(eng, stages, n, width, lags):
            def step(t, j):
                for lag, body in stages:
                    if not isinstance(t, int) or 0 <= t - lag < n:
                        body(t - lag, (j - lag) % width)

            fill = width * ((lags + width - 1) // width + 1)
            for t in range(fill):
                step(t, t % width)
            if n // width - 1 > fill // width:
                with eng.Fori(fill // width, n // width - 1) as i:
                    for j in range(width):
                        step(i * width + j, j)
            for t in range(max(fill, n - width), n + lags):
                step(t, t % width)

        def mm(o, l, r, start=True, stop=True):
            return nc.tensor.matmul(o, l, r, start=start, stop=stop, skip_group_check=True)

        def tr(o, i, n=P):
            return nc.tensor.transpose(o, i, ident[0:n, 0:n])

        small_q = [(ident, c_ident), (wv_s, Wv), (wq_s, Wq), (wo_s, Wo)]
        small_x = [(wk_s, Wk), (headmask, c_head)]
        small_s = [(sw_q, w_q), (sw_k, w_k), (sw_v, w_v), (same, c_same), (earlier, c_earlier),
                   (rank, c_rank), (wg_s, Wg)]
        N_Q = 16 * (len(small_q) + 3 + 1)
        N_X = 16 * len(small_x)
        N_S = 16 * (len(small_s) + 1 + NG)

        @block.sync
        def _(sp):
            for j in range(NLX):
                n = NT // NLX
                sp.dma_start(X[:, j * n:(j + 1) * n, :], x_tiles[:, j * n:(j + 1) * n, :]).then_inc(ld_x[j], 16)

            for dst, src in small_x:
                sp.dma_start(dst[:, :], src).then_inc(ld_wx, 16)

            def load_batch(i, b, first):
                if not first:
                    sp.wait_ge(pe_l, i * BT + (b - BT + 1))
                sp.dma_start(CX[:, b, :, :], ctx_in[bass.ds(i * BT + b, 1), 0:KC * P, :]
                             .rearrange("a (j p) c -> p (a j) c", p=P)).then_inc(ld_ctx[b], 16)
                sp.dma_start(CXE[0:1, b, :], ctx_in[bass.ds(i * BT + b, 1), KC * P, :]).then_inc(ld_ctx[b], 16)
                if not first:
                    sp.wait_ge(pool_m, i * BT + (b - BT + 1))
                sp.dma_start(MK[:, b, :],
                             mask[bass.ds(i * BT + b, 1), :, :].broadcast_to([4, SQ, S2])).then_inc(ld_mask[b], 16)

            for b in range(BT):
                load_batch(0, b, True)
            for dst, src in small_s:
                sp.dma_start(dst[:, :], src).then_inc(ld_s, 16)
            sp.dma_start(rope[:, :, :], c_rope.rearrange("p (a s) -> p a s", a=2)).then_inc(ld_s, 16)
            for g in range(NG):
                sp.dma_start(sw_o[g * 32:(g + 1) * 32, :],
                             w_o.rearrange("(k g d) c -> g k d c", k=NG, g=4)[g]).then_inc(ld_s, 16)

            def load_last_values(m, b, first):
                if not first:
                    sp.wait_ge(pe_o, m - (BT - 1))
                sp.dma_start(VE[:, b, :], v_last[bass.ds(m, 1), :, :].rearrange("a g c -> (a g) c"))\
                    .then_inc(ld_ve[b], 16)

            sp.wait_ge(st_vl, 16)
            for b in range(BT):
                load_last_values(b, b, True)

            def load_tile(i):
                for b in range(BT):
                    load_batch(i, b, False)
                    if b >= 2 or not isinstance(i, int):
                        load_last_values(i * BT + b - 2, (b - 2) % BT, False)

            load_tile(1)
            with sp.Fori(2, NT) as i:
                load_tile(i)
            for b in range(2, BT):
                load_last_values(NB - BT + b, b, False)
            sp.dma_start(w1_s[:, :, :], W1.rearrange("e c f -> c e f")).then_inc(ld_ffn, 16)
            sp.dma_start(w2_s[:, :, :, :], W2.rearrange("e (j f) c -> f e j c", f=P)).then_inc(ld_ffn, 16)
            def store(g):
                sp.dma_start(out_tiles[:, bass.ds(g * 4, 4), :], X[:, bass.ds(g * 4, 4), :]).then_inc(st_out, 16)

            for g in range(LATE):
                sp.wait_ge(f_late, (g + 1) * (4 * E))
                store(g)
            with sp.Fori(LATE, NT // 4) as g:
                sp.wait_ge(f_x, (g - (LATE - 1)) * (4 * E))
                store(g)
            sp.wait_ge(st_out, 16 * (NT // 4))

        @block.scalar
        def _(act):
            act.dma_start(CLAST, ctx_in[:, KC * P, :]).then_inc(ld_last, 16)
            for dst, src in small_q:
                act.dma_start(dst[:, :], src).then_inc(ld_q, 16)
            for j, bvec in enumerate((bq, bk, bv)):
                act.dma_start(bias[:, j:j + 1], bvec.rearrange("(c a) -> c a", a=1)).then_inc(ld_q, 16)
            act.dma_start(brow[:, :], bo.rearrange("(a c) -> a c", a=1)).then_inc(ld_q, 16)

            act.wait_ge(warm_ok, 1)

            GX = NT // NLX // 4

            def root(u, h):
                if u % GX == 0:
                    act.wait_ge(n0_std, u // GX + 1)
                    part = std[:, u * 4:(u + GX) * 4]
                    nc.scalar.activation(part, part, ACT.Sqrt).then_inc(n0_rstd, 1)

            def evac_x(u, h):
                act.wait_ge(n0_tr, u + 1)
                wait_reuse(act, n0_q, u - 1)
                nc.scalar.activation(xg[:, h, :], psum[h][:, :], ACT.Copy).then_inc(n0_xt, 1)

            def evac_q(u, h):
                act.wait_ge(n0_q, u + 1)
                nc.scalar.activation(QT[:, bass.ds(u * 512, 512)], psum[2 + h][:, :], ACT.Identity,
                                     bias=qbias[:, :], scale=-SCALE).then_inc(n0_qt, 1)

            for u in range(NT // 4 + 1):
                if u < NT // 4:
                    root(u, u % 2)
                    evac_x(u, u % 2)
                if u == 1:
                    act.wait_ge(n0_bias, 1)
                if u:
                    evac_q(u - 1, (u - 1) % 2)

            def evac_ctx(n, b):
                act.wait_ge(pe_l, n + 1)
                nc.scalar.activation(CT[:, b % 2, :], psum[0][:, 0:S2], ACT.Copy).then_inc(ev_l, 1)

            def evac_k(n, b):
                act.wait_ge(pe_k, n + 1)
                nc.scalar.activation(KH[:, b % 2, 0:S2], psum[1][:, 0:S2], ACT.Identity,
                                     bias=bias[:, 1:2]).then_inc(ev_k, 1)

            def exp_group(n, i, b, g):
                act.wait_ge(dve_min, 4 * n + (g + 1))
                nc.scalar.activation(PR[:, b % 2, g, :], SM[:, g, :], ACT.Exp, bias=MN[:, g:g + 1], scale=-1.0,
                                     accum_out=RSUM[:, bass.ds(i, 1), b, g:g + 1].rearrange("p a g -> p (a g)"))\
                    .then_inc(act_exp, 1)

            def evac_last_key(m, b):
                act.wait_ge(pe_e, m + 1)
                nc.scalar.activation(PTE[:, b % 2, :], psum[0][0:4, 3 * P:4 * P], ACT.Copy).then_inc(ev_e, 1)

            def evac_values(n, b, turned):
                act.wait_ge(pe_v, n + 1)
                if turned:
                    act.wait_ge(pe_e, n - 1)
                nc.scalar.activation(VT[:, b, :], psum[0][:, 0:KC * P], ACT.Copy).then_inc(ev_w, 1)

            def evac_out(q, half, first):
                act.wait_ge(pe_o, 2 * q + 2)
                if not first:
                    act.wait_ge(pool_o, q - 1)
                nc.scalar.activation(OC[:, half, :], psum[6][:, half * 2 * P:(half + 1) * 2 * P], ACT.Copy)\
                    .then_inc(ev_o, 1)

            def batch(i, b, more, first_tile, second_tile=False):
                n = i * BT + b
                nb = (b + 1) % BT
                exp_group(n, i, b, 0)
                if more:
                    evac_ctx(n + 1, nb)
                exp_group(n, i, b, 1)
                if more:
                    evac_k(n + 1, nb)
                exp_group(n, i, b, 2)
                exp_group(n, i, b, 3)
                if b % 2 == 1 and (b == 3 or not first_tile):
                    evac_out(i * 2 + (b - 3) // 2, int(b == 1), first_tile or (second_tile and b == 1))
                if more:
                    evac_values(n + 1, nb, not first_tile or b >= 1)
                if not first_tile or b >= 1:
                    evac_last_key(n - 1, (b - 1) % BT)

            nc.scalar.activation(warm[:, :], warm[:, :], ACT.Exp)
            evac_ctx(0, 0)
            evac_k(0, 0)
            evac_values(0, 0, False)
            act.wait_ge(vlm_ok, NG)
            act.dma_start(v_last, VLM[:, :, :]).then_inc(st_vl, 16)
            for b in range(BT):
                batch(0, b, True, True)
            for b in range(BT):
                batch(1, b, True, False, True)
            with act.Fori(2, NT - 1) as i:
                for b in range(BT):
                    batch(i, b, True, False)
            for b in range(BT):
                batch(NT - 1, b, b < BT - 1, False)
            evac_last_key(NB - 1, BT - 1)
            evac_out(NB // 2 - 1, 1, False)

            def spread(t, j):
                wait_reuse(act, pe_r, t - 3)
                nc.scalar.activation(
                    RIE[:, j, :].rearrange("p (g k d) -> p g k d", g=NG, k=4),
                    RIN[:, :, bass.ds(t, 1), :].rearrange("p k a g -> p g k a")
                    .broadcast_to([P, NG, 4, HD]), ACT.Copy).then_inc(act_spread, 1)

            def evac_inverse(t, j):
                act.wait_ge(pe_r, t + 1)
                wait_reuse(act, pool_otn, t - 3)
                nc.scalar.activation(RTO[:, j, :], psum[j][:, 0:P], ACT.Copy).then_inc(act_r, 1)

            act.wait_ge(dve_rs, 1)
            pipeline(act, [(0, spread), (1, evac_inverse)], NT, 4, 4)

            act.wait_ge(ld_ffn, 32)
            act.wait_ge(pool_o, NB // 2)
            nc.scalar.activation(W1H[:, :, :], w1_s[:, :, :], ACT.Copy).then_inc(w1_h, 1)

            act.wait_ge(n1_std, 1)
            nc.scalar.activation(std[:, :], std[:, :], ACT.Sqrt).then_inc(n1_rstd, 1)

            nc.scalar.activation(warm[:, :], warm[:, :], ACT.Exp)

            def centre(t, j):
                wait_reuse(act, a_tr, t - 3)
                nc.scalar.activation(xn[:, 0, j, :], X[:, bass.ds(t, 1), :].rearrange("p a c -> p (a c)"), ACT.Identity,
                                     bias=shift[:, bass.ds(t, 1)], scale=rstd[:, bass.ds(t, 1)]).then_inc(a_xn, 1)

            def evac_xt(t, j):
                act.wait_ge(a_tr, t + 1)
                wait_reuse(act, a_v, t - 3)
                nc.scalar.activation(xt[:, j, :], psum[0][:, 0:P], ACT.Copy).then_inc(a_xt, 1)

            def exp_scores(t, j):
                act.wait_ge(a_sx, t + 1)
                nc.scalar.activation(SX[:, j, :, :], SX[:, j, :, :], ACT.Exp, scale=SCALE).then_inc(a_ex, 1)

            def evac_probs(t, j):
                act.wait_ge(a_pt, t + 1)
                wait_reuse(act, a_o, t - 3)
                nc.scalar.activation(SP[:, j, :, :].rearrange("p b k -> p (b k)"), psum[6][:, :],
                                     ACT.Copy).then_inc(a_sp, 1)

            def evac_o(t, j):
                act.wait_ge(a_o, t + 1)
                wait_reuse(act, a_wo, t - 3)
                nc.scalar.activation(SO[:, j, :], psum[7][:, 0:P], ACT.Copy).then_inc(a_so, 1)

            def own_values(t, j):
                act.wait_ge(a_v, t + 1)
                wait_reuse(act, a_o, t - 3)
                for g in range(NG):
                    rows = slice(g * 32, g * 32 + 32)
                    last = nc.scalar.activation(VB[rows, j, :, g, :],
                                                psum[1][rows, 0:P].rearrange("p (b k d) -> p b k d", b=BT, k=NG)
                                                [:, :, g, :], ACT.Copy)
                last.then_inc(a_vb, 1)

            def own_keys(t, j):
                act.wait_ge(a_qk, t + 1)
                wait_reuse(act, a_s, t - 3)
                for g in range(NG):
                    rows = slice(g * 32, g * 32 + 32)
                    last = nc.scalar.activation(KB[rows, j, :, g, :],
                                                QKR[rows, j, 1, :].rearrange("p (b k) -> p b k", b=BT), ACT.Copy)
                last.then_inc(a_kb, 1)

            act.wait_ge(zero_ok, 1)
            act.wait_ge(n1_shift, 1)
            centre(0, 0)
            pipeline(act, [(5, evac_probs), (2, own_keys), (0, evac_xt), (3, exp_scores), (5, evac_o), (1, own_values),
                           (-1, centre)], NT, 4, 6)

            act.wait_ge(n2_std, 1)
            nc.scalar.activation(std[:, :], std[:, :], ACT.Sqrt).then_inc(n2_rstd, 1)

            def evac_router(u, h):
                act.wait_ge(r_tr, u + 1)
                wait_reuse(act, r_lg, u - 1)
                wait_reuse(act, r_xl, u - 1)
                nc.scalar.activation(xg[:, h, :], psum[h][:, :], ACT.Copy).then_inc(r_xt, 1)
                nc.scalar.activation(XH[:, bass.ds(u * 512, 512)], psum[h][:, :], ACT.Copy).then_inc(r_xh, 1)

            pipeline(act, [(0, evac_router)], NT // 4, 2, 2)
            act.wait_ge(t_act, 1)
            nc.scalar.activation(PRB[:, :, :], PRB[:, :, :], ACT.Exp).then_inc(t_exp, 1)

            nc.scalar.activation(warm[:, :], warm[:, :], ACT.Gelu)
            def gelu(i, e):
                u = i * E + e
                for j in range(FC):
                    act.wait_ge(f_h, u * FC + (j + 1))
                    if j == 0 and not (isinstance(u, int) and u < 2):
                        act.wait_ge(f_y, u - 1)
                    nc.scalar.activation(HT[e % 2][j], psum[2 * (e % 2) + j][:, :], ACT.Gelu)\
                        .then_inc(f_g, 1)

            def keep(i, e):
                act.wait_ge(f_y, i * E + e + 1)
                nc.scalar.activation(KEPT[i][e], psum[4 + e % 2][:, :], ACT.Copy).then_inc(f_keep, 1)

            for u in range(LATE * E):
                gelu(u // E, u % E)
                if u:
                    keep((u - 1) // E, (u - 1) % E)
            keep(LATE - 1, E - 1)
            with act.Fori(LATE, NT // 4) as i:
                for e in range(E):
                    gelu(i, e)

        @block.gpsimd
        def _(pool):
            nc.gpsimd.memset(warm[:, :], 0.0).then_inc(warm_ok, 1)
            nc.gpsimd.memset(VLM[:, :, :], 0.0).then_inc(vlm_zero, 1)
            nc.gpsimd.memset(ones1[:, :], 1.0).then_inc(ones_ok, 1)
            nc.gpsimd.memset(zero_row[:, :], 0.0)
            nc.gpsimd.memset(KH[:, :, S2:SE].bitcast(F32), 0.0)
            nc.gpsimd.memset(KL[:, :, S2:SE].bitcast(F32), 0.0).then_inc(kpad, 1)
            nc.gpsimd.memset(KB[:, :, :, :, :], 0.0)
            nc.gpsimd.memset(VB[:, :, :, :, :], 0.0).then_inc(zero_ok, 1)

            pool.wait_ge(ld_wx, N_X)
            pool.wait_ge(n0_qt, NT // 4)

            def prepare(n, b, first):
                if not first:
                    pool.wait_ge(pe_s, 4 * n - 12)
                    pool.wait_ge(dve_min, 4 * n - 12)
                pool.wait_ge(ld_mask[b], 16 // BT * (n - b) + 16)
                queries = QT[:, bass.ds(n * SQ, SQ)].rearrange("p (a q) -> p a q", a=1).broadcast_to([P, 4, SQ])
                own = headmask[:, :].rearrange("p (a h) -> p h a", a=1).broadcast_to([P, 4, SQ])
                nc.gpsimd.tensor_tensor(QB[:, b % 2, :, :], queries, own, ALU.mult).then_inc(pool_b, 1)
                nc.gpsimd.tensor_tensor(QH[:, b, :, :], queries, own, ALU.mult).then_inc(pool_b, 1)
                pool.wait_ge(pool_b, 2 * n + 2)
                nc.gpsimd.tensor_tensor(QL[:, b, :, :], QB[:, b % 2, :, :], QH[:, b, :, :],
                                        ALU.subtract).then_inc(pool_q, 1)
                nc.gpsimd.tensor_scalar(MB[:, b, :], MK[:, b, :], 0.0, BIG, ALU.is_equal, ALU.mult)\
                    .then_inc(pool_m, 1)

            def keep_own(q, k):
                pool.wait_ge(ev_o, q + 1)
                own = OC[:, k, :].rearrange("p (s h q) -> p s h q", s=2, h=4)
                for s in range(2):
                    nc.gpsimd.tensor_tensor(
                        own[:, s], own[:, s],
                        headmask[:, :].rearrange("p (a h) -> p h a", a=1).broadcast_to([P, 4, SQ]),
                        ALU.mult).then_inc(pool_c, 1)
                pool.wait_ge(pool_c, 4 * q + 2)
                nc.gpsimd.tensor_tensor(own[:, :, 0:2], own[:, :, 0:2], own[:, :, 2:4], ALU.add).then_inc(pool_c, 2)
                pool.wait_ge(pool_c, 4 * q + 4)
                nc.gpsimd.tensor_tensor(OT[:, bass.ds(q * 2 * SQ, 2 * SQ)].rearrange("p (s q) -> p s q", s=2),
                                        own[:, :, 0], own[:, :, 1], ALU.add).then_inc(pool_o, 1)

            def tile(i):
                for b in range(BT):
                    n = i * BT + b
                    prepare(n, b, isinstance(i, int) and i == 0)
                    if b % 2 == 1 and not (isinstance(i, int) and n < 5):
                        keep_own(i * 2 + (b - 5) // 2, int(b == 3))

            tile(0)
            pool.wait_ge(brow_sp, 1)
            nc.gpsimd.tensor_tensor(X[:, :, :], X[:, :, :],
                                    BROW[:, :].rearrange("p (a c) -> p a c", a=1).broadcast_to([P, NT, P]),
                                    ALU.add).then_inc(x_biased, 1)
            tile(1)
            with pool.Fori(2, NT) as i:
                tile(i)
            keep_own(NB // 2 - 2, 0)
            keep_own(NB // 2 - 1, 1)

            def normalise_out(t, j):
                pool.wait_ge(act_r, t + 1)
                wait_reuse(pool, pe_x1, t - 3)
                nc.gpsimd.tensor_tensor(OTN[:, j, :], OT[:, bass.ds(t * P, P)], RTO[:, j, :],
                                        ALU.mult).then_inc(pool_otn, 1)

            pool.wait_ge(pool_o, NB // 2)
            pipeline(pool, [(0, normalise_out)], NT, 4, 4)

            pool.wait_ge(w1_h, 1)
            nc.gpsimd.tensor_tensor(W1L[:, :, :], w1_s[:, :, :], W1H[:, :, :], ALU.subtract).then_inc(w1_l, 1)

            def rotate(t, j):
                pool.wait_ge(a_tq, 2 * t + 2)
                wait_reuse(pool, a_s, t - 3)
                nc.gpsimd.tensor_tensor(QKR[:, j, :, :], TQ[:, j, 0::2, :], TQ[:, j, 1::2, :], ALU.add)\
                    .then_inc(a_qk, 1)

            def spread_queries(t, j):
                pool.wait_ge(a_qk, t + 1)
                nc.gpsimd.tensor_tensor(
                    QD[:, j, :, :, :],
                    QKR[:, j, 0, :].rearrange("p (b a q) -> p b a q", b=BT, a=1).broadcast_to([P, BT, 4, SQ]),
                    headmask[:, :].rearrange("p (a h c) -> p a h c", a=1, c=1).broadcast_to([P, BT, 4, SQ]),
                    ALU.mult).then_inc(a_qd, 1)

            def normalise_probs(t, j):
                pool.wait_ge(a_inv, t + 1)
                nc.gpsimd.tensor_tensor(
                    SX[:, j, :, :], SX[:, j, :, :],
                    sinv[:, j, :].rearrange("p (n a) -> p n a", a=1).broadcast_to([P, 16, SQ]),
                    ALU.mult).then_inc(a_pn, 1)

            pipeline(pool, [(2, rotate), (4, normalise_probs), (2, spread_queries)], NT, 4, 6)

            def input_rest(u, h):
                pool.wait_ge(r_xh, u + 1)
                nc.gpsimd.tensor_tensor(XL[:, bass.ds(u * 512, 512)], xg[:, h, :],
                                        XH[:, bass.ds(u * 512, 512)], ALU.subtract).then_inc(r_xl, 1)

            pipeline(pool, [(0, input_rest)], NT // 4, 2, 2)


        @block.tensor
        def _(pe):
            pe.wait_ge(ld_q, N_Q)
            pe.wait_ge(ld_last, 16)
            tr(psum[6][:, 0:P], CLAST).then_inc(pe_clt, 1)

            mm(psum[4][0:1, 0:P], bias[:, 2:3], wo_s[:, :]).then_inc(brow_pe, 1)
            pe.wait_ge(ones_ok, 1)
            pe.wait_ge(brow_ok, 1)
            mm(psum[5][:, 0:P], ones1[0:1, :], brow[0:1, :]).then_inc(brow_all, 1)

            def turn_norm(u, h):
                wait_reuse(pe, n0_xt, u - 1)
                for j in range(4):
                    pe.wait_ge(n0_xn, 4 * u + (j + 1))
                    last = tr(psum[h][:, j * P:(j + 1) * P], xn[:, h, j, :])
                last.then_inc(n0_tr, 1)

            def queries(u, h):
                pe.wait_ge(n0_xt, u + 1)
                wait_reuse(pe, n0_qt, u - 1)
                mm(psum[2 + h][:, :], wq_s[:, :], xg[:, h, :]).then_inc(n0_q, 1)

            pipeline(pe, [(0, turn_norm), (1, queries)], NT // 4, 2, 2)

            def ctx_transpose(n, i, b, first):
                pe.wait_ge(ld_ctx[b % BT], 32 * i + 32)
                if not first:
                    pe.wait_ge(ev_w, n)
                    wait_reuse(pe, ev_e, n - 2)
                for j in range(KC):
                    tr(psum[0][:, j * P:(j + 1) * P], CX[:, b % BT, j, :])
                tr(psum[0][:, KC * P:S2], CXE[0:1, b % BT, :], 1).then_inc(pe_l, 1)

            def keys(n, b, first):
                pe.wait_ge(ev_l, n + 1)
                if not first:
                    pe.wait_ge(ev_kl, n)
                mm(psum[1][:, 0:S2], wk_s[:, :], CT[:, b % 2, :]).then_inc(pe_k, 1)

            def values(n, b):
                pe.wait_ge(ev_l, n + 1)
                for j in range(KC):
                    last = mm(psum[0][:, j * P:(j + 1) * P], CT[:, b % 2, j * P:(j + 1) * P], wv_s[:, :])
                last.then_inc(pe_v, 1)

            def energies(n, b, first):
                pe.wait_ge(ev_k, n + 1)
                pe.wait_ge(pool_q, n + 1)
                for g in range(NG):
                    rows = slice(32 * g, 32 * g + 32)
                    if not first:
                        pe.wait_ge(dve_min, 4 * n + (g - 3))
                    for k, (q_part, k_part) in enumerate(((QH, KH), (QL, KH), (QH, KL))):
                        if g == 0 and k_part is KL:
                            pe.wait_ge(ev_kl, n + 1)
                        last = mm(psum[2 + g][:, 0:SE], q_part[rows, b, :, :].rearrange("p h q -> p (h q)"),
                                  k_part[rows, b % 2, :], start=(k == 0), stop=(k == 2))
                    last.then_inc(pe_s, 1)

            def turn(m, b, half, first):
                pe.wait_ge(act_exp, 4 * m + (2 * half + 2))
                if first and half == 0:
                    pe.wait_ge(vlm_ok, NG)
                if not first:
                    pe.wait_ge(ev_t, 2 * m + half)
                for k in range(2):
                    for j in range(KC):
                        col = (k * KC + j) * P
                        last = tr(psum[7][:, col:col + P], PR[:, b % 2, 2 * half + k, j * P:(j + 1) * P])
                last.then_inc(pe_t, 1)

            def turn_last_key(m, b):
                pe.wait_ge(act_exp, 4 * m + 4)
                tr(psum[0][0:4, 3 * P:4 * P], PR[:, b % 2, :, KC * P]).then_inc(pe_e, 1)

            def attend(m, b, pairs_out):
                pe.wait_ge(ev_t, 2 * m + 2)
                pe.wait_ge(ev_w, m + 1)
                if pairs_out is not None:
                    pe.wait_ge(ev_o, pairs_out)
                for j in range(KC):
                    for g in range(NG):
                        last = mm(psum[6][32 * g:32 * g + 32, b * P:(b + 1) * P],
                                  VT[:, b, j * P + 32 * g:j * P + 32 * g + 32],
                                  PT[:, b % 2, g, j * P:(j + 1) * P], start=(j == 0), stop=False)
                last.then_inc(pe_a, 1)

            def attend_last_key(m, b, i):
                pe.wait_ge(ev_e, m + 1)
                pe.wait_ge(ld_ve[b], 16 * i + 16)
                mm(psum[6][:, b * P:(b + 1) * P], VE[:, b, :], PTE[:, b % 2, :], start=False)\
                    .then_inc(pe_o, 1)

            def step(i, b, more):
                n = i * BT + b
                m, pb = n - 1, (b - 1) % BT
                start = isinstance(n, int) and n < BT
                prev = not (start and n < 1)
                nb, ni = (b + 1) % BT, i + (b + 1) // BT
                energies(n, b, start and n == 0)
                if more:
                    ctx_transpose(n + 1, ni, nb, False)
                if prev:
                    turn(m, pb, 0, start and m == 0)
                if not (start and n < 2):
                    attend(n - 2, (b - 2) % BT, i * 2 + (b - 2) // 2 if b % 2 == 0 and not start else None)
                if more:
                    keys(n + 1, nb, False)
                if not (start and n < 2):
                    attend_last_key(n - 2, (b - 2) % BT, i + (b - 2) // BT)
                if prev:
                    turn(m, pb, 1, False)
                if more:
                    values(n + 1, nb)
                if prev:
                    turn_last_key(m, pb)

            pe.wait_ge(n0_qt, NT // 4)
            pe.wait_ge(brow_sp, 1)
            pe.wait_ge(kpad, 1)
            pe.wait_ge(ld_wx, N_X)
            ctx_transpose(0, 0, 0, True)
            keys(0, 0, True)
            values(0, 0)
            pe.wait_ge(dve_clt, 1)
            mm(psum[7][:, 0:P], CLT, wv_s[:, :]).then_inc(pe_vl, 1)
            for b in range(BT):
                step(0, b, True)
            with pe.Fori(1, NT - 1) as i:
                for b in range(BT):
                    step(i, b, True)
            for b in range(BT):
                step(NT - 1, b, b < BT - 1)
            m = NB - 1
            turn(m, BT - 1, 0, False)
            attend(m - 1, BT - 2, NB // 2 - 1)
            attend_last_key(m - 1, BT - 2, NT - 1)
            turn(m, BT - 1, 1, False)
            pe.wait_ge(ev_e, m)
            turn_last_key(m, BT - 1)
            attend(m, BT - 1, None)
            attend_last_key(m, BT - 1, NT - 1)

            pe.wait_ge(ev_t, 2 * NB)
            pe.wait_ge(dve_inv, NT)
            for k in range(4):
                for b in range(BT):
                    last = mm(psum[k][32 * b:32 * b + 32, 0:NT * NG],
                              ident[32 * k:32 * k + 32, 32 * k:32 * k + 32],
                              RSUM[32 * k:32 * k + 32, :, b, :])
            last.then_inc(pe_rs, 1)
            pe.wait_ge(dve_rs, 1)
            pe.wait_ge(ev_o, NB // 2)

            def turn_inverse(t, j):
                pe.wait_ge(act_spread, t + 1)
                wait_reuse(pe, act_r, t - 3)
                tr(psum[j][:, 0:P], RIE[:, j, :]).then_inc(pe_r, 1)

            def out_project(t, j):
                pe.wait_ge(pool_otn, t + 1)
                wait_reuse(pe, dve_x1, t - 3)
                mm(psum[4 + j][:, 0:P], OTN[:, j, :], wo_s[:, :]).then_inc(pe_x1, 1)

            pipeline(pe, [(0, turn_inverse), (2, out_project)], NT, 4, 4)

            pe.wait_ge(wqk_ok, 1)
            pe.wait_ge(ld_s, N_S)
            pe.wait_ge(dve_x1, NT)

            def turn_x(t, j):
                pe.wait_ge(a_xn, t + 1)
                wait_reuse(pe, a_xt, t)
                tr(psum[0][:, 0:P], xn[:, 0, j, :]).then_inc(a_tr, 1)

            def project(t, j):
                pe.wait_ge(a_xt, t + 1)
                wait_reuse(pe, a_tq, 2 * t - 2)
                for w in range(4):
                    last = mm(psum[2 + j % 2][:, w * P:(w + 1) * P], wqk[:, w, :], xt[:, j, :])
                last.then_inc(a_p, 1)

            def self_values(t, j):
                wait_reuse(pe, a_vb, t)
                for b in range(BT):
                    for g in range(4):
                        last = mm(psum[1][32 * g:32 * g + 32, 32 * b:32 * b + 32],
                                  xt[:, j, b * SQ:(b + 1) * SQ], sw_v[:, :])
                last.then_inc(a_v, 1)

            def scores(t, j):
                pe.wait_ge(a_kb, t + 1)
                pe.wait_ge(a_qd, t + 1)
                wait_reuse(pe, a_sx, t - 1)
                for b in range(BT):
                    last = mm(psum[4 + j % 2][:, b * P:(b + 1) * P],
                              QD[:, j, b, :, :].rearrange("p h q -> p (h q)"),
                              KB[:, j, b, :, :].rearrange("p h q -> p (h q)"))
                last.then_inc(a_s, 1)

            def turn_probs(t, j):
                pe.wait_ge(a_pn, t + 1)
                wait_reuse(pe, a_sp, t)
                for b in range(BT):
                    last = tr(psum[6][:, b * P:(b + 1) * P],
                              SX[:, j, 4 * b:4 * b + 4, :].rearrange("p n k -> p (n k)"))
                last.then_inc(a_pt, 1)

            def weigh_values(t, j):
                pe.wait_ge(a_sp, t + 1)
                pe.wait_ge(a_vb, t + 1)
                wait_reuse(pe, a_x2, t)
                for b in range(BT):
                    for g in range(4):
                        last = mm(psum[7][32 * g:32 * g + 32, b * SQ:(b + 1) * SQ],
                                  VB[:, j, b, :, :].rearrange("p h d -> p (h d)"),
                                  SP[:, j, b, g * SQ:(g + 1) * SQ])
                last.then_inc(a_o, 1)

            def project_out(t, j):
                pe.wait_ge(a_so, t + 1)
                mm(psum[7][:, P:2 * P], SO[:, j, :], sw_o[:, :]).then_inc(a_wo, 1)

            pipeline(pe, [(3, scores), (6, project_out), (1, project), (0, turn_x), (5, weigh_values),
                          (1, self_values), (4, turn_probs)], NT, 4, 6)

            pe.wait_ge(a_x2, NT)

            def turn_router(u, h):
                wait_reuse(pe, r_xh, u - 1)
                for j in range(4):
                    pe.wait_ge(r_xn, 4 * u + (j + 1))
                    last = tr(psum[h][:, j * P:(j + 1) * P], xn[:, h, j, :])
                last.then_inc(r_tr, 1)

            def logits(u, h):
                pe.wait_ge(r_xt, u + 1)
                wait_reuse(pe, r_cp, u - 1)
                for j in range(4):
                    last = mm(psum[2 + h][:, j * E:(j + 1) * E], xg[:, h, j * P:(j + 1) * P], wg_s[:, :])
                last.then_inc(r_lg, 1)

            pipeline(pe, [(0, turn_router), (1, logits)], NT // 4, 2, 2)

            pe.wait_ge(ld_ffn, 32)
            pe.wait_ge(w1_l, 1)
            pe.wait_ge(r_xl, NT // 4)
            pe.wait_ge(r_cp, NT // 4)

            def hidden(i, e):
                u = i * E + e
                for j in range(FC):
                    if not (isinstance(u, int) and u < 2):
                        pe.wait_ge(f_g, (u - 2) * FC + (j + 1))
                    for k, (w_part, x_part) in enumerate(((W1H, XL), (W1L, XH), (W1H, XH))):
                        last = mm(psum[2 * (e % 2) + j][:, :], w_part[:, e, j * P:(j + 1) * P],
                                  x_part[:, bass.ds(i * 512, 512)], start=(k == 0), stop=(k == 2))
                    last.then_inc(f_h, 1)

            def expand(i, e):
                u = i * E + e
                pe.wait_ge(f_g, u * FC + FC)
                if not (isinstance(u, int) and u < 2):
                    if isinstance(u, int) and u - 2 < LATE * E:
                        pe.wait_ge(f_keep, u - 1)
                    else:
                        pe.wait_ge(f_x, 4 * (u - (LATE * E + 1)))
                for t in range(4):
                    for j in range(FC):
                        last = mm(psum[4 + e % 2][:, t * P:(t + 1) * P], HT[e % 2][j][:, t * P:(t + 1) * P],
                                  w2_s[:, e, j, :], start=(j == 0), stop=(j == FC - 1))
                last.then_inc(f_y, 1)

            nb = len(bits)

            def router_step(k):
                pe.wait_ge(t_dve, k + 1)
                if k == 0:
                    for a in range(HALVES):
                        last = tr(psum[6][:, a * P:(a + 1) * P],
                                  PRB[:, a * 16:(a + 1) * 16, :].rearrange("p i e -> p (i e)"))
                elif k <= nb + 1:
                    last = mm(psum[7][:, 0:1], same[:, :], cnt[:, :])
                elif k == nb + 2:
                    for a in range(HALVES):
                        for c in range(a + 1):
                            last = mm(psum[7][:, a:a + 1], earlier[:, :] if c == a else same[:, :],
                                      tot[:, c:c + 1], start=(c == 0), stop=(c == a))
                else:
                    for a in range(HALVES):
                        last = tr(psum[6][:, a * P:(a + 1) * P], GT[:, a, :])
                last.then_inc(t_pe, 1)

            steps = nb + 4
            k = 0
            for u in range(LATE * E):
                if u % E == 0:
                    hidden(u // E, 0)
                if u % E + 1 < E:
                    hidden(u // E, u % E + 1)
                if k < steps:
                    router_step(k)
                    k += 1
                expand(u // E, u % E)
                if k < steps:
                    router_step(k)
                    k += 1

            def group(i, more):
                hidden(i, 0)
                for e in range(E):
                    if e + 1 < E:
                        hidden(i, e + 1)
                    if more and e < more:
                        router_step(steps - more + e)
                    expand(i, e)

            group(LATE, steps - k)
            with pe.Fori(LATE + 1, NT // 4) as i:
                group(i, 0)

        @block.vector
        def _(dve):
            V = nc.vector
            chain = [0]

            def link(ins):
                chain[0] += 1
                ins.then_inc(dve_c, 1)
                dve.wait_ge(dve_c, chain[0])

            def moments_to_rstd(st_sem, rs_sem, count=1, tiles=slice(0, NT), done=None):
                me, mo = stats[:, tiles, 1], stats[:, tiles, 4]
                V.tensor_tensor(mv[:, tiles, 0], me, mo, ALU.add).then_inc(dve_c, 1)
                V.tensor_tensor(mv[:, tiles, 1], me, mo, ALU.subtract).then_inc(dve_c, 1)
                V.tensor_tensor(std[:, tiles], stats[:, tiles, 2], stats[:, tiles, 5], ALU.add).then_inc(dve_c, 1)
                chain[0] += 3
                dve.wait_ge(dve_c, chain[0])
                V.tensor_tensor(mv[:, tiles, 1], mv[:, tiles, 1], mv[:, tiles, 1], ALU.mult).then_inc(dve_c, 1)
                V.tensor_scalar(std[:, tiles], std[:, tiles], 1.0 / D, EPS, ALU.mult, ALU.add).then_inc(dve_c, 1)
                V.tensor_scalar(mv[:, tiles, 0], mv[:, tiles, 0], 0.5, None, ALU.mult).then_inc(dve_c, 1)
                chain[0] += 3
                dve.wait_ge(dve_c, chain[0])
                V.scalar_tensor_tensor(std[:, tiles], mv[:, tiles, 1], 0.25, std[:, tiles], ALU.mult, ALU.add).then_inc(st_sem, 1)
                dve.wait_ge(rs_sem, count)
                link(V.reciprocal(rstd[:, tiles], std[:, tiles]))
                if done is not None:
                    V.scalar_tensor_tensor(shift[:, tiles], mv[:, tiles, 0], -1.0, rstd[:, tiles], ALU.mult, ALU.mult)\
                        .then_inc(done, 1)

            def normalise(dst, src, tile):
                return V.tensor_scalar(dst, src,
                                       mv[:, bass.ds(tile, 1), 0], rstd[:, bass.ds(tile, 1)],
                                       ALU.subtract, ALU.mult)

            link(V.memset(thr[:, :], 1 << bits[0]))
            TX = NT // NLX

            def norm_queries(u, h):
                wait_reuse(dve, n0_tr, u - 1)
                for j in range(4):
                    t = u * 4 + j
                    normalise(xn[:, h, j, :], X[:, t, :], t).then_inc(n0_xn, 1)

            for q in range(NLX):
                dve.wait_ge(ld_x[q], 16)
                with dve.Fori(q * TX // 4, (q + 1) * TX // 4) as i:
                    for j in range(4):
                        V.bn_stats(stats[:, bass.ds(i * 4 + j, 1), :].rearrange("p a s -> p (a s)"),
                                   X[:, bass.ds(i * 4 + j, 1), :].rearrange("p a c -> p (a c)"))\
                            .then_inc(dve_st1, 1)
                dve.wait_ge(dve_st1, (q + 1) * TX)
                moments_to_rstd(n0_std, n0_rstd, q + 1, slice(q * TX, (q + 1) * TX))
                if q == 1:
                    dve.wait_ge(brow_all, 1)
                    V.tensor_copy(BROW[:, :], psum[5][:, 0:P]).then_inc(brow_sp, 1)
                    dve.wait_ge(pe_clt, 1)
                    V.tensor_copy(CLT, psum[6][:, 0:P]).then_inc(dve_clt, 1)
                if q == 0:
                    dve.wait_ge(ld_q, N_Q)
                    V.tensor_scalar(qbias[:, :], bias[:, 0:1], -SCALE, None, ALU.mult).then_inc(n0_bias, 1)
                    dve.wait_ge(brow_pe, 1)
                    V.tensor_tensor(brow[:, :], brow[:, :], psum[4][0:1, 0:P], ALU.add).then_inc(brow_ok, 1)
                for u in range(q * TX // 4, (q + 1) * TX // 4):
                    norm_queries(u, u % 2)
            dve.wait_ge(ld_s, N_S)
            qv = sw_q[:, :].rearrange("p (h a f) -> p h a f", h=NG * 4, a=2)
            kv = sw_k[:, :].rearrange("p (k g a f) -> p k g a f", k=NG, g=1, a=2)
            for a in range(2):
                for w, s in ((0, a), (1, 1 - a)):
                    V.tensor_copy(wqk[:, w, :].rearrange("p (h a f) -> p h a f", h=NG * 4, a=2)[:, :, a, :],
                                  qv[:, :, s, :])
                    last = V.tensor_copy(
                        wqk[:, 2 + w, :].rearrange("p (k g a f) -> p k g a f", k=NG, g=4, a=2)[:, :, :, a, :],
                        kv[:, :, :, s, :].broadcast_to([P, NG, 4, 4]))
            last.then_inc(wqk_ok, 1)

            def mask_min(n, b, g, first):
                dve.wait_ge(pe_s, 4 * n + (g + 1))
                if g == 0:
                    dve.wait_ge(pool_m, n + 1)
                if not first:
                    dve.wait_ge(act_exp, 4 * n + (g - 3))
                V.memset(waited[:, g:g + 1], 0.0)
                V.tensor_tensor_reduce(SM[:, g, :], psum[2 + g][:, 0:S2], MB[:, b, :], 1.0, float(3e38),
                                       ALU.add, ALU.min, MN[:, g:g + 1]).then_inc(dve_min, 1)

            def evac_turned(m, b, half, first):
                dve.wait_ge(pe_t, 2 * m + (half + 1))
                if half == 0 and not first:
                    dve.wait_ge(pe_a, m - 1)
                V.tensor_copy(PT[:, b % 2, 2 * half:2 * half + 2, :].rearrange("p g k -> p (g k)"),
                              psum[7][:, :]).then_inc(ev_t, 1)

            def key_rest(n, b):
                dve.wait_ge(ev_k, n + 1)
                V.scalar_tensor_tensor(KL[:, b % 2, 0:S2], psum[1][:, 0:S2], bias[:, 1:2], KH[:, b % 2, 0:S2],
                                       ALU.add, ALU.subtract).then_inc(ev_kl, 1)

            def invert_tile_sums(i):
                dve.wait_ge(act_exp, 4 * BT * i + 4 * BT)
                sums = RSUM[:, bass.ds(i, 1), :, :].rearrange("p a b g -> p (a b g)")
                V.reciprocal(sums, sums).then_inc(dve_inv, 1)

            def batch(i, b, more=True):
                n = i * BT + b
                start = isinstance(n, int)
                if b == 1 and not (start and n < BT):
                    invert_tile_sums(i - 1)
                for g in range(NG):
                    mask_min(n, b, g, start and n == 0)
                if not (start and n < 1):
                    evac_turned(n - 1, (b - 1) % BT, 0, start and n < 3)
                if more:
                    key_rest(n + 1, (b + 1) % BT)
                if not (start and n < 1):
                    evac_turned(n - 1, (b - 1) % BT, 1, start and n < 3)

            key_rest(0, 0)
            dve.wait_ge(pe_vl, 1)
            dve.wait_ge(vlm_zero, 1)
            for g in range(NG):
                V.tensor_copy(VLM[:, g, g * 32:(g + 1) * 32], psum[7][:, g * 32:(g + 1) * 32])\
                    .then_inc(vlm_ok, 1)
            for b in range(BT):
                batch(0, b)
            with dve.Fori(1, NT - 1) as i:
                for b in range(BT):
                    batch(i, b)
            for b in range(BT):
                batch(NT - 1, b, b < BT - 1)
            for half in range(2):
                evac_turned(NB - 1, BT - 1, half, False)

            invert_tile_sums(NT - 1)

            dve.wait_ge(pe_rs, 1)
            for k in range(4):
                last = V.tensor_copy(RIN[:, k, :, :].rearrange("p i g -> p (i g)"), psum[k][:, 0:NT * NG])
            last.then_inc(dve_rs, 1)
            dve.wait_ge(x_biased, 1)

            def cross_residual(t, j):
                dve.wait_ge(pe_x1, t + 1)
                xi = X[:, bass.ds(t, 1), :].rearrange("p a c -> p (a c)")
                V.tensor_tensor(xi, xi, psum[4 + j][:, 0:P], ALU.add).then_inc(dve_x1, 1)

            def cross_statistics(t, j):
                dve.wait_ge(dve_x1, t + 1)
                V.bn_stats(stats[:, bass.ds(t, 1), :].rearrange("p a s -> p (a s)"),
                           X[:, bass.ds(t, 1), :].rearrange("p a c -> p (a c)")).then_inc(dve_st1, 1)

            pipeline(dve, [(0, cross_residual), (1, cross_statistics)], NT, 4, 4)
            dve.wait_ge(dve_st1, 2 * NT)
            moments_to_rstd(n1_std, n1_rstd, done=n1_shift)

            def rotary(t, j):
                dve.wait_ge(a_p, t + 1)
                wait_reuse(dve, a_qk, t - 3)
                for w in range(2):
                    V.tensor_tensor(
                        TQ[:, j, w::2, :].rearrange("p w (b s) -> p w b s", b=BT),
                        psum[2 + j % 2][:, :].rearrange("p (w b s) -> p w b s", w=4, b=BT)[:, w::2],
                        rope[:, w, :].rearrange("p (c d s) -> p c d s", c=1, d=1)
                        .broadcast_to([P, 2, BT, SQ]), ALU.mult).then_inc(a_tq, 1)

            def shift_scores(t, j):
                dve.wait_ge(a_s, t + 1)
                V.tensor_reduce(smx[:, j, :], psum[4 + j % 2][:, :].rearrange("p (n k) -> p n k", n=16), AX_X,
                                ALU.max).then_inc(a_mx, 1)
                wait_reuse(dve, a_pt, t - 3)
                dve.wait_ge(a_mx, t + 1)
                V.tensor_tensor(SX[:, j, :, :], psum[4 + j % 2][:, :].rearrange("p (n k) -> p n k", n=16),
                                smx[:, j, :].rearrange("p (n a) -> p n a", a=1).broadcast_to([P, 16, SQ]),
                                ALU.subtract).then_inc(a_sx, 1)

            def sum_probs(t, j):
                dve.wait_ge(a_ex, t + 1)
                V.tensor_reduce(ssum[:, j, :], SX[:, j, :, :], AX_X, ALU.add).then_inc(a_sum, 1)

            def invert_sums(t, j):
                dve.wait_ge(a_sum, t + 1)
                V.reciprocal(sinv[:, j, :], ssum[:, j, :]).then_inc(a_inv, 1)

            def residual(t, j):
                dve.wait_ge(a_wo, t + 1)
                xi = X[:, bass.ds(t, 1), :].rearrange("p a c -> p (a c)")
                V.tensor_tensor(xi, xi, psum[7][:, P:2 * P], ALU.add).then_inc(a_x2, 1)

            def statistics(t, j):
                dve.wait_ge(a_x2, t + 1)
                V.bn_stats(stats[:, bass.ds(t, 1), :].rearrange("p a s -> p (a s)"),
                           X[:, bass.ds(t, 1), :].rearrange("p a c -> p (a c)")).then_inc(a_st, 1)

            pipeline(dve, [(4, sum_probs), (4, invert_sums), (6, residual), (3, shift_scores), (6, statistics),
                           (1, rotary)], NT, 4, 6)
            dve.wait_ge(a_st, NT)
            moments_to_rstd(n2_std, n2_rstd)

            def norm_router(u, h):
                wait_reuse(dve, r_tr, u - 1)
                for j in range(4):
                    t = u * 4 + j
                    normalise(xn[:, h, j, :], X[:, bass.ds(t, 1), :].rearrange("p a c -> p (a c)"), t)\
                        .then_inc(r_xn, 1)

            def keep_logits(u, h):
                dve.wait_ge(r_lg, u + 1)
                V.tensor_copy(PRB[:, bass.ds(u * 4, 4), :].rearrange("p i e -> p (i e)"),
                              psum[2 + h][:, 0:4 * E]).then_inc(r_cp, 1)

            pipeline(dve, [(0, norm_router), (2, keep_logits)], NT // 4, 2, 2)
            dve.wait_ge(r_cp, NT // 4)

            def over_experts(v):
                return v.rearrange("p (i a) -> p i a", a=1).broadcast_to([P, NT, E])

            link(V.tensor_reduce(rmx[:, :], PRB[:, :, :], AX_X, ALU.max))
            V.tensor_tensor(PRB[:, :, :], PRB[:, :, :], over_experts(rmx[:, :]), ALU.subtract).then_inc(t_act, 1)
            dve.wait_ge(t_exp, 1)
            link(V.tensor_reduce(rmx[:, :], PRB[:, :, :], AX_X, ALU.add))
            link(V.reciprocal(any_[:, :], rmx[:, :]))
            V.tensor_tensor(PRB[:, :, :], PRB[:, :, :], over_experts(any_[:, :]), ALU.mult).then_inc(t_dve, 1)
            dve.wait_ge(t_pe, 1)
            link(V.tensor_copy(PRT[:, :, :].rearrange("p a t -> p (a t)"), psum[6][:, 0:HALVES * P]))
            def bit_next(bit):
                return (1 << bit) >> 1

            prt = PRT[:, :, :].rearrange("p a t -> p (a t)")
            cmpf = cmp_[:, :, :].rearrange("p a t -> p (a t)")

            for k, bit in enumerate(bits):
                V.tensor_scalar(cmpf, prt, thr[:, :].bitcast(F32), 0.0, ALU.is_ge, ALU.add,
                                accum_out=cnt[:, :]).then_inc(t_dve, 1)
                nxt = V.tensor_scalar(thr_next[:, :], thr[:, :], bit_next(bit), None, ALU.bitwise_xor)
                nxt.then_inc(dve_c, 1)
                chain[0] += 1
                dve.wait_ge(t_pe, 2 + k)
                link(V.tensor_scalar(bit_off[:, :], psum[7][:, 0:1], CAP - 0.5, float(1 << bit),
                                     ALU.is_lt, ALU.mult))
                link(V.tensor_tensor(thr[:, :], thr_next[:, :], bit_off[:, :], ALU.bitwise_xor))
            nb = len(bits)
            thf = thr[:, :].bitcast(F32)
            V.tensor_scalar(GT[:, :, :].rearrange("p a t -> p (a t)"), prt, thf, 0.0, ALU.is_gt, ALU.add,
                            accum_out=cnt[:, :]).then_inc(t_dve, 1)
            dve.wait_ge(t_pe, 2 + nb)
            link(V.tensor_scalar(need[:, 0:1], psum[7][:, 0:1], -1.0, float(CAP), ALU.mult, ALU.add))
            for a in range(HALVES):
                link(V.tensor_scalar(EQ[:, a, :], PRT[:, a, :], thf, 0.0, ALU.is_equal, ALU.add,
                                     accum_out=tot[:, a:a + 1]))
            V.memset(cmpf, 0.0).then_inc(t_dve, 1)
            dve.wait_ge(t_pe, 3 + nb)
            link(V.tensor_copy(need[:, 1:2], need[:, 0:1]))
            link(V.tensor_tensor(need[:, :], need[:, :], psum[7][:, 0:HALVES], ALU.subtract))
            for a in range(HALVES):
                link(V.tensor_tensor_scan(PFX[:, a, :], EQ[:, a, :], zero_row[:, :], 0.0, ALU.add, ALU.add))
                link(V.tensor_scalar(PFX[:, a, :], PFX[:, a, :], need[:, a:a + 1], None, ALU.is_le))
            link(V.tensor_tensor(PFX[:, :, :], PFX[:, :, :], EQ[:, :, :], ALU.mult))
            V.tensor_tensor(GT[:, :, :], GT[:, :, :], PFX[:, :, :], ALU.add).then_inc(t_dve, 1)
            dve.wait_ge(t_pe, 4 + nb)
            link(V.tensor_copy(SEL[:, :, :].rearrange("p i e -> p (i e)"), psum[6][:, 0:HALVES * P]))
            link(V.tensor_tensor(KEY[:, :, :], PRB[:, :, :], SEL[:, :, :], ALU.mult))
            link(V.tensor_scalar(RT[:, :, :], SEL[:, :, :], -1.0, None, ALU.add))
            link(V.tensor_tensor(KEY[:, :, :], KEY[:, :, :], RT[:, :, :], ALU.add))
            link(V.tensor_reduce(any_[:, :], KEY[:, :, :], AX_X, ALU.max))
            link(V.tensor_scalar(rmx[:, :], any_[:, :], 0.0, None, ALU.is_lt))
            link(V.tensor_scalar(any_[:, :], any_[:, :], 0.0, None, ALU.is_ge))
            link(V.tensor_tensor(KEY[:, :, :], KEY[:, :, :], over_experts(any_[:, :]), ALU.mult))
            link(V.tensor_tensor(RT[:, :, :], PRB[:, :, :], over_experts(rmx[:, :]), ALU.mult))
            link(V.tensor_tensor(KEY[:, :, :], KEY[:, :, :], RT[:, :, :], ALU.add))
            link(V.tensor_reduce(rmx[:, :], KEY[:, :, :], AX_X, ALU.max))
            link(V.tensor_tensor(KEY[:, :, :], KEY[:, :, :], over_experts(rmx[:, :]), ALU.is_equal))
            by_rank = rank[:, :].rearrange("p (a e) -> p a e", a=1).broadcast_to([P, NT, E])
            link(V.tensor_tensor(KEY[:, :, :], KEY[:, :, :], by_rank, ALU.mult))
            link(V.tensor_reduce(rmx[:, :], KEY[:, :, :], AX_X, ALU.max))
            link(V.tensor_tensor(KEY[:, :, :], by_rank, over_experts(rmx[:, :]), ALU.is_equal))
            V.tensor_tensor(GATE[:, :, :], KEY[:, :, :], PRB[:, :, :], ALU.mult).then_inc(t_done, 1)
            dve.wait_ge(t_done, 1)

            def add(i, e, outputs, done):
                for t in range(4):
                    xi = X[:, bass.ds(i * 4 + t, 1), :].rearrange("p a c -> p (a c)")
                    V.scalar_tensor_tensor(xi, outputs[:, t * P:(t + 1) * P],
                                           GATE[:, bass.ds(i * 4 + t, 1), e], xi, ALU.mult, ALU.add)\
                        .then_inc(done, 1)

            def add_next(i, e):
                u = i * E + e
                dve.wait_ge(f_y, u + 1)
                if e:
                    dve.wait_ge(f_x, 4 * (u - LATE * E))
                add(i, e, psum[4 + e % 2], f_x)

            dve.wait_ge(f_keep, LATE * E)
            for i in range(LATE):
                for e in range(E):
                    add_next(LATE + i, e)
                    if e:
                        dve.wait_ge(f_late, 4 * (i * E + e))
                    add(i, e, KEPT[i][e], f_late)
            with dve.Fori(2 * LATE, NT // 4) as i:
                for e in range(E):
                    add_next(i, e)


_INS = ["x", "ctx_1024", "mask_BxSxS2_ik1", "L0_xattn_Wq", "L0_xattn_bq", "L0_xattn_Wk", "L0_xattn_bk",
        "L0_xattn_Wv", "L0_xattn_bv", "L0_xattn_Wo", "L0_xattn_bo", "L0_attn_w_q", "L0_attn_w_k",
        "L0_attn_w_v", "L0_attn_w_o", "L0_ffn_Wg", "L0_ffn_W1", "L0_ffn_W2"]


def kernel(**inputs):
    import concourse.bacc as bacc
    from concourse.bass_utils import run_bass_kernel_spmd

    nc = bacc.Bacc("TRN2", target_bir_lowering=False, num_devices=1)
    arrays, args = {}, []
    for name in _INS:
        a = np.ascontiguousarray(inputs[name])
        arrays["in_" + name] = a
        args.append(nc.dram_tensor("in_" + name, a.shape, mybir.dt.from_np(a.dtype), kind="ExternalInput").ap())
    B, S, D = inputs["x"].shape
    table = shape_constants(B, S)
    for name in _CONSTS:
        a = np.ascontiguousarray(table[name])
        arrays["const_" + name] = a
        args.append(nc.dram_tensor("const_" + name, a.shape, F32, kind="ExternalInput").ap())
    args.append(nc.dram_tensor("out", (B, S, D), F32, kind="ExternalOutput").ap())
    perceiver_block(nc, *args)
    r = run_bass_kernel_spmd(nc, [arrays], core_ids=[0])
    return r.results[0]["out"]
```
